# Optimizing a Trainium2 kernel written in Bass

```python
import numpy as np
import jax
import jax.numpy as jnp

def _softmax(x, axis=-1):
    return jax.nn.softmax(x, axis=axis)

def _gelu(x):
    return jax.nn.gelu(x, approximate=True)

def _silu(x):
    return jax.nn.silu(x)

def _sigmoid(x):
    return jax.nn.sigmoid(x)

def _layernorm(x, axis=-1, eps=1e-05):
    m = jnp.mean(x, axis=axis, keepdims=True)
    v = jnp.var(x, axis=axis, keepdims=True)
    return (x - m) / jnp.sqrt(v + eps)

def _scatter_add(tgt, idx, src, axis=0):
    return tgt.at[idx].add(src)

def _segment_sum(src, seg, n):
    return jax.ops.segment_sum(src, seg, n)
kernel_name = 'mk_dlrm_tower_d1_rec_r8_437481'

def setup_inputs(seed: int=0):
    np.random.seed(seed)
    _w = jnp.asarray

    def _rec_inputs():
        import jax
        import jax.numpy as jnp
        _tk = jax.random.key(seed)
        dense_ctx = jax.random.normal(jax.random.fold_in(_tk, 190), (512, 16), jnp.float32)
        ids = jnp.stack([jax.random.randint(jax.random.fold_in(_tk, 200 + f), (512,), 0, v, jnp.int32) for f, v in enumerate([125000, 12500, 12500, 12500, 1000, 1250, 1250, 1000, 1250, 12500, 1000, 1000, 1000, 125000, 12500, 125000, 1000, 1250, 1000, 12500, 1000, 1000, 1250, 1000, 1250, 1250, 12500, 1250, 1000, 1250, 12500, 1000])], axis=1)
        tbl_0 = 0.05 * jax.random.normal(jax.random.fold_in(_tk, 500 + 0), (125000, 64), jnp.float32)
        tbl_1 = 0.05 * jax.random.normal(jax.random.fold_in(_tk, 500 + 1), (12500, 64), jnp.float32)
        tbl_2 = 0.05 * jax.random.normal(jax.random.fold_in(_tk, 500 + 2), (12500, 64), jnp.float32)
        tbl_3 = 0.05 * jax.random.normal(jax.random.fold_in(_tk, 500 + 3), (12500, 64), jnp.float32)
        tbl_4 = 0.05 * jax.random.normal(jax.random.fold_in(_tk, 500 + 4), (1000, 64), jnp.float32)
        tbl_5 = 0.05 * jax.random.normal(jax.random.fold_in(_tk, 500 + 5), (1250, 64), jnp.float32)
        tbl_6 = 0.05 * jax.random.normal(jax.random.fold_in(_tk, 500 + 6), (1250, 64), jnp.float32)
        tbl_7 = 0.05 * jax.random.normal(jax.random.fold_in(_tk, 500 + 7), (1000, 64), jnp.float32)
        tbl_8 = 0.05 * jax.random.normal(jax.random.fold_in(_tk, 500 + 8), (1250, 64), jnp.float32)
        tbl_9 = 0.05 * jax.random.normal(jax.random.fold_in(_tk, 500 + 9), (12500, 64), jnp.float32)
        tbl_10 = 0.05 * jax.random.normal(jax.random.fold_in(_tk, 500 + 10), (1000, 64), jnp.float32)
        tbl_11 = 0.05 * jax.random.normal(jax.random.fold_in(_tk, 500 + 11), (1000, 64), jnp.float32)
        tbl_12 = 0.05 * jax.random.normal(jax.random.fold_in(_tk, 500 + 12), (1000, 64), jnp.float32)
        tbl_13 = 0.05 * jax.random.normal(jax.random.fold_in(_tk, 500 + 13), (125000, 64), jnp.float32)
        tbl_14 = 0.05 * jax.random.normal(jax.random.fold_in(_tk, 500 + 14), (12500, 64), jnp.float32)
        tbl_15 = 0.05 * jax.random.normal(jax.random.fold_in(_tk, 500 + 15), (125000, 64), jnp.float32)
        tbl_16 = 0.05 * jax.random.normal(jax.random.fold_in(_tk, 500 + 16), (1000, 64), jnp.float32)
        tbl_17 = 0.05 * jax.random.normal(jax.random.fold_in(_tk, 500 + 17), (1250, 64), jnp.float32)
        tbl_18 = 0.05 * jax.random.normal(jax.random.fold_in(_tk, 500 + 18), (1000, 64), jnp.float32)
        tbl_19 = 0.05 * jax.random.normal(jax.random.fold_in(_tk, 500 + 19), (12500, 64), jnp.float32)
        tbl_20 = 0.05 * jax.random.normal(jax.random.fold_in(_tk, 500 + 20), (1000, 64), jnp.float32)
        tbl_21 = 0.05 * jax.random.normal(jax.random.fold_in(_tk, 500 + 21), (1000, 64), jnp.float32)
        tbl_22 = 0.05 * jax.random.normal(jax.random.fold_in(_tk, 500 + 22), (1250, 64), jnp.float32)
        tbl_23 = 0.05 * jax.random.normal(jax.random.fold_in(_tk, 500 + 23), (1000, 64), jnp.float32)
        tbl_24 = 0.05 * jax.random.normal(jax.random.fold_in(_tk, 500 + 24), (1250, 64), jnp.float32)
        tbl_25 = 0.05 * jax.random.normal(jax.random.fold_in(_tk, 500 + 25), (1250, 64), jnp.float32)
        tbl_26 = 0.05 * jax.random.normal(jax.random.fold_in(_tk, 500 + 26), (12500, 64), jnp.float32)
        tbl_27 = 0.05 * jax.random.normal(jax.random.fold_in(_tk, 500 + 27), (1250, 64), jnp.float32)
        tbl_28 = 0.05 * jax.random.normal(jax.random.fold_in(_tk, 500 + 28), (1000, 64), jnp.float32)
        tbl_29 = 0.05 * jax.random.normal(jax.random.fold_in(_tk, 500 + 29), (1250, 64), jnp.float32)
        tbl_30 = 0.05 * jax.random.normal(jax.random.fold_in(_tk, 500 + 30), (12500, 64), jnp.float32)
        tbl_31 = 0.05 * jax.random.normal(jax.random.fold_in(_tk, 500 + 31), (1000, 64), jnp.float32)
        _rk = jax.random.fold_in(_tk, 7)
        W_top1 = 0.0441942 * jax.random.normal(jax.random.fold_in(_tk, 801), (512, 512), jnp.float32)
        W_top2 = 0.0441942 * jax.random.normal(jax.random.fold_in(_tk, 802), (512, 256), jnp.float32)
        W_top3 = 0.0625 * jax.random.normal(jax.random.fold_in(_tk, 803), (256, 1), jnp.float32)
        b_top1 = jnp.zeros((512,), jnp.float32)
        b_top2 = jnp.zeros((256,), jnp.float32)
        return (dense_ctx, ids, tbl_0, tbl_1, tbl_2, tbl_3, tbl_4, tbl_5, tbl_6, tbl_7, tbl_8, tbl_9, tbl_10, tbl_11, tbl_12, tbl_13, tbl_14, tbl_15, tbl_16, tbl_17, tbl_18, tbl_19, tbl_20, tbl_21, tbl_22, tbl_23, tbl_24, tbl_25, tbl_26, tbl_27, tbl_28, tbl_29, tbl_30, tbl_31, W_top1, b_top1, W_top2, b_top2, W_top3)
    dense_ctx, ids, tbl_0, tbl_1, tbl_2, tbl_3, tbl_4, tbl_5, tbl_6, tbl_7, tbl_8, tbl_9, tbl_10, tbl_11, tbl_12, tbl_13, tbl_14, tbl_15, tbl_16, tbl_17, tbl_18, tbl_19, tbl_20, tbl_21, tbl_22, tbl_23, tbl_24, tbl_25, tbl_26, tbl_27, tbl_28, tbl_29, tbl_30, tbl_31, W_top1, b_top1, W_top2, b_top2, W_top3 = _rec_inputs()

    def _L0_rec_setup():
        import jax, jax.numpy as jnp
        import numpy as np
        FIELDS = 32
        EMBED = 64
        PAIRS = FIELDS * (FIELDS - 1) // 2
        BATCH = 256
        key = jax.random.key(seed)
        k1, k2 = jax.random.split(key)
        x = jax.random.normal(k1, (BATCH, FIELDS, EMBED), dtype=jnp.float32)
        kernel = jax.random.normal(k2, (EMBED, PAIRS, EMBED), dtype=jnp.float32) * 0.05
        return {'x': x, 'kernel': kernel}
    _L0_rec_all = _L0_rec_setup()
    _L0_rec_in = {k: v for k, v in _L0_rec_all.items() if k in ('kernel',)}
    del _L0_rec_all
    return {'dense_ctx': dense_ctx, 'ids': ids, 'tbl_0': tbl_0, 'tbl_1': tbl_1, 'tbl_2': tbl_2, 'tbl_3': tbl_3, 'tbl_4': tbl_4, 'tbl_5': tbl_5, 'tbl_6': tbl_6, 'tbl_7': tbl_7, 'tbl_8': tbl_8, 'tbl_9': tbl_9, 'tbl_10': tbl_10, 'tbl_11': tbl_11, 'tbl_12': tbl_12, 'tbl_13': tbl_13, 'tbl_14': tbl_14, 'tbl_15': tbl_15, 'tbl_16': tbl_16, 'tbl_17': tbl_17, 'tbl_18': tbl_18, 'tbl_19': tbl_19, 'tbl_20': tbl_20, 'tbl_21': tbl_21, 'tbl_22': tbl_22, 'tbl_23': tbl_23, 'tbl_24': tbl_24, 'tbl_25': tbl_25, 'tbl_26': tbl_26, 'tbl_27': tbl_27, 'tbl_28': tbl_28, 'tbl_29': tbl_29, 'tbl_30': tbl_30, 'tbl_31': tbl_31, 'W_top1': W_top1, 'b_top1': b_top1, 'W_top2': W_top2, 'b_top2': b_top2, 'W_top3': W_top3, 'L0_rec_kernel': _L0_rec_in['kernel']}

def reference(dense_ctx, ids, tbl_0, tbl_1, tbl_2, tbl_3, tbl_4, tbl_5, tbl_6, tbl_7, tbl_8, tbl_9, tbl_10, tbl_11, tbl_12, tbl_13, tbl_14, tbl_15, tbl_16, tbl_17, tbl_18, tbl_19, tbl_20, tbl_21, tbl_22, tbl_23, tbl_24, tbl_25, tbl_26, tbl_27, tbl_28, tbl_29, tbl_30, tbl_31, W_top1, b_top1, W_top2, b_top2, W_top3, L0_rec_kernel):
    import jax
    import jax.numpy as jnp

    def _L0_rec_ref(x, kernel):
        import jax, jax.numpy as jnp
        import numpy as np
        FIELDS = 32
        EMBED = 64
        PAIRS = FIELDS * (FIELDS - 1) // 2
        BATCH = 256
        iu, ju = jnp.triu_indices(FIELDS, k=1)
        p = x[:, iu, :]
        q = x[:, ju, :]
        result = jnp.einsum('bpe,fpe,bpf->bp', p, kernel, q)
        return result
    e = jnp.stack([tbl_0[ids[:, 0]], tbl_1[ids[:, 1]], tbl_2[ids[:, 2]], tbl_3[ids[:, 3]], tbl_4[ids[:, 4]], tbl_5[ids[:, 5]], tbl_6[ids[:, 6]], tbl_7[ids[:, 7]], tbl_8[ids[:, 8]], tbl_9[ids[:, 9]], tbl_10[ids[:, 10]], tbl_11[ids[:, 11]], tbl_12[ids[:, 12]], tbl_13[ids[:, 13]], tbl_14[ids[:, 14]], tbl_15[ids[:, 15]], tbl_16[ids[:, 16]], tbl_17[ids[:, 17]], tbl_18[ids[:, 18]], tbl_19[ids[:, 19]], tbl_20[ids[:, 20]], tbl_21[ids[:, 21]], tbl_22[ids[:, 22]], tbl_23[ids[:, 23]], tbl_24[ids[:, 24]], tbl_25[ids[:, 25]], tbl_26[ids[:, 26]], tbl_27[ids[:, 27]], tbl_28[ids[:, 28]], tbl_29[ids[:, 29]], tbl_30[ids[:, 30]], tbl_31[ids[:, 31]]], axis=1)
    z = _L0_rec_ref(e, L0_rec_kernel)
    z = z.reshape(z.shape[0], -1)
    h = jnp.concatenate([z, dense_ctx], axis=1)
    h = jnp.maximum(h @ W_top1 + b_top1, 0.0)
    h = jnp.maximum(h @ W_top2 + b_top2, 0.0)
    y = h @ W_top3
    return y

_drawn_inputs = setup_inputs


def setup_inputs(seed=0):
    import zlib

    import numpy as np

    out = dict(_drawn_inputs(seed))
    spreads = {'b_top1': (0.0, 0.1), 'b_top2': (0.0, 0.1)}
    factors = {'tbl_0': 6.658,
     'tbl_1': 6.055,
     'tbl_2': 5.746,
     'tbl_3': 5.832,
     'tbl_4': 4.95,
     'tbl_5': 6.513,
     'tbl_6': 5.69,
     'tbl_7': 5.001,
     'tbl_8': 5.216,
     'tbl_9': 5.757,
     'tbl_10': 5.578,
     'tbl_11': 5.78,
     'tbl_12': 5.437,
     'tbl_13': 5.076,
     'tbl_14': 6.158,
     'tbl_15': 5.742,
     'tbl_16': 5.375,
     'tbl_17': 5.756,
     'tbl_18': 4.929,
     'tbl_19': 5.691,
     'tbl_20': 5.404,
     'tbl_21': 5.953,
     'tbl_22': 5.928,
     'tbl_23': 5.596,
     'tbl_24': 6.173,
     'tbl_25': 5.558,
     'tbl_26': 5.836,
     'tbl_27': 5.573,
     'tbl_28': 6.15,
     'tbl_29': 5.679,
     'tbl_30': 5.709,
     'tbl_31': 6.16}
    for name, (base, spread) in spreads.items():
        noise = np.random.default_rng([zlib.crc32(name.encode()), seed]).standard_normal(out[name].shape)
        drawn = base * np.exp(spread * noise) if base else spread * noise
        out[name] = jnp.asarray(drawn.astype(out[name].dtype))
    for name, factor in factors.items():
        out[name] = (out[name] * factor).astype(out[name].dtype)
    return out
```

```python
from contextlib import ExitStack

import numpy as np

import concourse.bass as bass
from concourse import mybir
from concourse.alu_op_type import AluOpType as ALU

F32 = mybir.dt.float32
F32R = mybir.dt.float32r
I32 = mybir.dt.int32
ACT = mybir.ActivationFunctionType
AX_X = mybir.AxisListType.X

P = 128
FIELDS = 32
E = 64
PAIRS = FIELDS * (FIELDS - 1) // 2
UNIT = 16
QUAD = 4
SLOTS = 16
V_SLOTS = 3
P_SLOTS = 3
K_SLOTS = 4
AHEAD = 2


def plan():
    def unit(side, ks, js):
        pairs = [(2 * side * k + i, 2 * side * k + side + j) for k in ks for j in js for i in range(side)]
        return dict(side=side, ks=list(ks), js=list(js), pairs=pairs)

    sq4 = [unit(4, [k], range(4)) for k in range(4)]
    sq8 = [[unit(8, [k], (2 * q, 2 * q + 1)) for q in range(4)] for k in range(2)]
    sq2 = [unit(2, range(4 * h, 4 * h + 4), range(2)) for h in range(2)]
    sq1 = [unit(1, range(8 * h, 8 * h + 8), range(1)) for h in range(2)]
    sq16 = [unit(16, [0], [j]) for j in range(16)]
    order = ([sq4[0], sq4[1], sq2[0], sq8[0][0], sq1[0]] + sq8[0][1:]
             + sq16[:8] + [sq4[2]] + sq16[8:] + [sq4[3], sq2[1], sq1[1]]
             + [sq8[1][2], sq8[1][3], sq8[1][0], sq8[1][1]])
    full = [u for u in order if len(u["pairs"]) == UNIT]
    groups = [full[n:n + 2] for n in range(0, len(full), 2)]
    groups.insert(2, sq1)
    at = 0
    for g, group in enumerate(groups):
        for u in group:
            u["at"], u["group"] = at, g
            at += len(u["pairs"])
    assert at == PAIRS
    return order, groups


ORDER, GROUPS = plan()
UNITS = len(ORDER)
STORED = [pair for group in GROUPS for u in group for pair in u["pairs"]]
TRIU = {(i, j): i * (2 * FIELDS - i - 1) // 2 + j - i - 1 for i in range(FIELDS) for j in range(i + 1, FIELDS)}
STORED_TO_TRIU = np.array([TRIU[pair] for pair in STORED])
FIRST_USE = {q: min(n for n, u in enumerate(ORDER) if any(j // QUAD == q for _, j in u["pairs"])) for q in range(8)}
LAST_USE = {q: max(n for n, u in enumerate(ORDER) if any(j // QUAD == q for _, j in u["pairs"])) for q in range(8)}
QUADS = sorted(range(8), key=lambda q: (FIRST_USE[q], q))
QUAD_AT = {q: max(0, FIRST_USE[q] - AHEAD) for q in QUADS}


def interaction_tower(nc, ids, dense, tables, k_raw, w1, b1, w2, b2, w3, y):
    tiles = dense.shape[0] // P
    zd = PAIRS + dense.shape[1]
    h1_dim, h2_dim = w1.shape[-1], w2.shape[-1]
    c0, c1, c2 = zd // P, h1_dim // P, h2_dim // P
    last_unit = tiles * UNITS

    with ExitStack() as ctx:
        def sb(name, shape, dt=F32):
            return ctx.enter_context(nc.sbuf_tensor(name, shape, dt))

        def psum(name, shape):
            return ctx.enter_context(nc.psum_tensor(name, shape, F32))

        def sem(name):
            return ctx.enter_context(nc.semaphore(name))

        kk = sb("kk", [P, PAIRS * E], F32R)
        emb = [sb(f"emb{i}", [P, FIELDS, E]) for i in range(2)]
        twice = sb("twice", [P, 2, QUAD, 2, E])
        xh = sb("xh", [P, SLOTS, P], F32R)
        xl = sb("xl", [P, SLOTS, P], F32R)
        prod = sb("prod", [P, P_SLOTS, UNIT * E])
        room = sb("room", [P, K_SLOTS, UNIT * E])
        k_high = sb("k_high", [P, 2, UNIT * E], F32R)
        z = [sb(f"z{i}", [P, zd]) for i in range(2)]
        zT = sb("zT", [P, c0, P])
        h1T = sb("h1T", [P, c1, P])
        h2T = zT[:, 0:c2, :]
        y_row = sb("y_row", [1, tiles * P])
        idx = sb("idx", [P, tiles * FIELDS], I32)
        ident = sb("ident", [P, P])
        b1_sb = sb("b1_sb", [P, c1])
        b2_sb = sb("b2_sb", [P, c2])
        w3_sb = sb("w3_sb", [P, c2])
        flat_room = room[:, :, :].rearrange("p a b -> p (a b)")
        w1_sb = flat_room[:, 0:c0 * h1_dim].rearrange("p (c n) -> p c n", c=c0)
        w2_sb = flat_room[:, c0 * h1_dim:c0 * h1_dim + c1 * h2_dim].rearrange("p (c n) -> p c n", c=c1)

        v = [psum(f"v{i}", [P, UNIT * E]) for i in range(V_SLOTS)]
        pT = psum("pT", [P, QUAD, P])
        pM = psum("pM", [P, 4 * P])

        ids_in = sem("ids_in")
        ident_zero, ident_ready = sem("ident_zero"), sem("ident_ready")
        gathered = [[sem(f"gathered{h}_{g}") for g in range(4)] for h in range(2)]
        k_in = [sem(f"k_in{i}") for i in range(K_SLOTS)]
        k_rounded = sem("k_rounded")
        k_high_placed = sem("k_high_placed")
        k_low = sem("k_low")
        k_moved = [sem(f"k_moved{i}") for i in range(K_SLOTS)]
        small_in = sem("small_in")
        w_in = sem("w_in")
        dense_in = [sem(f"dense_in{i}") for i in range(2)]
        quad_doubled, quad_transposed = sem("quad_doubled"), sem("quad_transposed")
        quad_high, quad_low = sem("quad_high"), sem("quad_low")
        v_ready = sem("v_ready")
        products = sem("products")
        sums = sem("sums")
        z_turned, zT_ready = sem("z_turned"), sem("zT_ready")
        h1_ready, h1T_ready = sem("h1_ready"), sem("h1T_ready")
        h2_ready, h2T_ready = sem("h2_ready"), sem("h2T_ready")
        y_ready, y_copied = sem("y_ready"), sem("y_copied")
        y_out = sem("y_out")

        def group_cols(g):
            return sum(len(u["pairs"]) for u in GROUPS[g]) * E // 2

        def placed(g, half, side):
            n = len(GROUPS[g][0]["pairs"]) * E
            at = GROUPS[g][0]["at"] * E
            both = kk[64 * side:64 * side + 64, at:at + 2 * n].rearrange("p (u h c) -> p u h c", u=2, h=2)
            return both[:, :, half, :]

        def packed(buf, g, half):
            return buf[64 * half:64 * half + 64, 0:group_cols(g)].rearrange("p (u c) -> p u c", u=2)

        def quads_before(n):
            return [q for q in QUADS if QUAD_AT[q] == n]

        block = ctx.enter_context(nc.Block())

        @block.sync
        def _(sp):
            sp.dma_start(idx[:, :], ids).then_inc(ids_in, 16)

            def load_k(g):
                cols = group_cols(g)
                at = GROUPS[g][0]["at"] * E // 2
                sp.dma_start(room[:, g % K_SLOTS, 0:cols], k_raw[:, at:at + cols]).then_inc(k_in[g % K_SLOTS], 16)

            def load_dense(t):
                sp.dma_start(z[t % 2][:, PAIRS:zd], dense[t * P:(t + 1) * P, :]).then_inc(dense_in[t % 2], 16)

            for g in range(K_SLOTS):
                load_k(g)
            sp.dma_start(b1_sb[:, :], b1).then_inc(small_in, 16)
            sp.dma_start(b2_sb[:, :], b2).then_inc(small_in, 16)
            sp.dma_start(w3_sb[:, :], w3).then_inc(small_in, 16)
            for g in range(len(GROUPS)):
                sp.wait_ge(k_low, g + 1)
                for half in range(2):
                    sp.dma_start(placed(g, half, 1 - half).bitcast(F32), packed(room[:, g % K_SLOTS, :], g, half)
                                 ).then_inc(k_moved[g % K_SLOTS], 16)
                if g >= 1 and g - 1 + K_SLOTS < len(GROUPS):
                    sp.wait_ge(k_moved[(g - 1) % K_SLOTS], 32 * ((g - 1) // K_SLOTS + 1))
                    load_k(g - 1 + K_SLOTS)
            for t in range(2):
                load_dense(t)
            for s in range(K_SLOTS):
                sp.wait_ge(k_moved[s], 32 * len(range(s, len(GROUPS), K_SLOTS)))
            sp.dma_start(w1_sb, w1).then_inc(w_in, 16)
            sp.dma_start(w2_sb, w2).then_inc(w_in, 16)
            for t in range(2, tiles):
                sp.wait_ge(z_turned, t - 1)
                load_dense(t)
            sp.wait_ge(y_copied, tiles)
            sp.dma_start(y, y_row[:, :]).then_inc(y_out, 16)
            sp.wait_ge(y_out, 16)

        @block.gpsimd
        def _(pool):
            nc.gpsimd.memset(ident[:, :], 0.0).then_inc(ident_zero, 1)
            pool.wait_ge(ident_zero, 1)
            nc.gpsimd.affine_select(out=ident[:, :], in_=ident[:, :], pattern=[[-1, P]], compare_op=ALU.not_equal,
                                    fill=1.0, base=0, channel_multiplier=1).then_inc(ident_ready, 1)
            pool.wait_ge(ids_in, 16)
            for t in range(tiles):
                if t >= 2:
                    pool.wait_ge(products, (t - 1) * UNITS)
                for f in range(FIELDS):
                    c = t * FIELDS + f
                    nc.gpsimd.indirect_dma_start(
                        emb[t % 2][:, f, :], None, tables[f],
                        bass.IndirectOffsetOnAxis(idx[:, c:c + 1], 0)).then_inc(gathered[t % 2][f // 8], 16)

        @block.tensor
        def _(pe):
            pe.wait_ge(ident_ready, 1)
            quads_done = [0]

            def transpose_quad(t, q):
                pe.wait_ge(quad_doubled, quads_done[0] + 1)
                pe.wait_ge(quad_low, quads_done[0])
                for r in range(QUAD):
                    x = twice[:, quads_done[0] % 2, r, :, :].rearrange("p a e -> p (a e)")
                    last = nc.tensor.transpose(pT[:, r, :], x, ident[:, :])
                last.then_inc(quad_transposed, 1)
                quads_done[0] += 1
                return quads_done[0]

            def unit(t, n, split_count):
                u = ORDER[n]
                count = t * UNITS + n
                if t == 0:
                    g = u["group"]
                    pe.wait_ge(k_high_placed, g + 1)
                    pe.wait_ge(k_moved[g % K_SLOTS], 32 * (g // K_SLOTS + 1))
                pe.wait_ge(quad_low, split_count)
                if count >= V_SLOTS:
                    pe.wait_ge(products, count - V_SLOTS + 1)
                out, at = v[count % V_SLOTS], u["at"] * E
                side, pos = u["side"], 0
                for k in u["ks"]:
                    for j in u["js"]:
                        slot = (2 * side * k + side + j) % SLOTS
                        width = side * E
                        pieces = [(pos + o, min(512, width)) for o in range(0, width, 512)]
                        for part in (xh, xl):
                            for o, w in pieces:
                                last = nc.tensor.matmul(out[:, o:o + w], part[:, slot, :], kk[:, at + o:at + o + w],
                                                        start=part is xh, stop=part is xl)
                        pos += width
                last.then_inc(v_ready, 1)

            def tower_transpose(t):
                pe.wait_ge(sums, (t + 1) * UNITS)
                pe.wait_ge(dense_in[t % 2], 16 * (t // 2 + 1))
                if t >= 1:
                    pe.wait_ge(y_copied, t)
                for c in range(c0):
                    last = nc.tensor.transpose(pM[:, c * P:(c + 1) * P], z[t % 2][:, c * P:(c + 1) * P], ident[:, :])
                last.then_inc(z_turned, 1)

            def dense_layer(w, x, chunks_in, chunks_out):
                for n in range(chunks_out):
                    for c in range(chunks_in):
                        last = nc.tensor.matmul(pM[:, n * P:(n + 1) * P], w[:, c, n * P:(n + 1) * P], x[:, c, :],
                                                start=c == 0, stop=c == chunks_in - 1)
                return last

            def tower_1(t):
                if t == 0:
                    pe.wait_ge(w_in, 32)
                pe.wait_ge(zT_ready, t + 1)
                dense_layer(w1_sb, zT, c0, c1).then_inc(h1_ready, 1)

            def tower_2(t):
                pe.wait_ge(h1T_ready, t + 1)
                dense_layer(w2_sb, h1T, c1, c2).then_inc(h2_ready, 1)

            def tower_3(t):
                pe.wait_ge(h2T_ready, t + 1)
                for c in range(c2):
                    last = nc.tensor.matmul(pM[0:1, 0:P], w3_sb[:, c:c + 1], h2T[:, c, :], start=c == 0, stop=c == c2 - 1)
                last.then_inc(y_ready, 1)

            tower = {3: tower_transpose, 5: tower_1, 7: tower_2, 9: tower_3}
            for t in range(tiles):
                split_at = {}
                for n in range(UNITS):
                    for q in quads_before(n):
                        split_at[q] = transpose_quad(t, q)
                    needed = {j // QUAD for _, j in ORDER[n]["pairs"]}
                    unit(t, n, max(split_at[q] for q in needed))
                    if t >= 1 and n in tower:
                        tower[n](t - 1)
            for n in sorted(tower):
                tower[n](tiles - 1)

        @block.scalar
        def _(act):
            def round_k(g):
                act.wait_ge(k_in[g % K_SLOTS], 16 * (g // K_SLOTS + 1))
                if g >= 2:
                    act.wait_ge(k_low, g - 1)
                cols = group_cols(g)
                nc.scalar.activation(k_high[:, g % 2, 0:cols], room[:, g % K_SLOTS, 0:cols], ACT.Copy
                                     ).then_inc(k_rounded, 1)
                act.wait_ge(k_rounded, g + 1)
                for half in range(2):
                    last = nc.scalar.activation(placed(g, half, half), packed(k_high[:, g % 2, :], g, half), ACT.Copy)
                last.then_inc(k_high_placed, 1)

            quads = [(t, q) for t in range(tiles) for q in QUADS]

            def double_quad(i):
                t, q = quads[i]
                act.wait_ge(gathered[t % 2][q // 2], 128 * (t // 2 + 1))
                if i >= 2:
                    act.wait_ge(quad_transposed, i - 1)
                x = emb[t % 2][:, QUAD * q:QUAD * q + QUAD, :].unsqueeze(2).broadcast_to([P, QUAD, 2, E])
                nc.scalar.activation(twice[:, i % 2, :, :, :], x, ACT.Copy).then_inc(quad_doubled, 1)

            quads_done = [0]

            def round_quad(t, q):
                if quads_done[0] + 1 < len(quads):
                    double_quad(quads_done[0] + 1)
                act.wait_ge(quad_transposed, quads_done[0] + 1)
                done = (t - 1) * UNITS + LAST_USE[q + 4] + 1 if q < 4 else t * UNITS + LAST_USE[q - 4] + 1
                if done > 0:
                    act.wait_ge(v_ready, done)
                s = QUAD * q % SLOTS
                nc.scalar.activation(xh[:, s:s + QUAD, :], pT[:, :, :], ACT.Copy).then_inc(quad_high, 1)
                quads_done[0] += 1

            def tower_transpose(t):
                act.wait_ge(z_turned, t + 1)
                nc.scalar.activation(zT[:, :, :], pM[:, 0:c0 * P].rearrange("p (c b) -> p c b", c=c0), ACT.Copy
                                     ).then_inc(zT_ready, 1)

            def relu_chunks(out, bias, chunks, done):
                for n in range(chunks):
                    last = nc.scalar.activation(out[:, n, :], pM[:, n * P:(n + 1) * P], ACT.Relu, bias=bias[:, n:n + 1])
                last.then_inc(done, 1)

            def tower_1(t):
                if t == 0:
                    act.wait_ge(small_in, 48)
                act.wait_ge(h1_ready, t + 1)
                relu_chunks(h1T, b1_sb, c1, h1T_ready)

            def tower_2(t):
                act.wait_ge(h2_ready, t + 1)
                relu_chunks(h2T, b2_sb, c2, h2T_ready)

            def tower_3(t):
                act.wait_ge(y_ready, t + 1)
                nc.scalar.activation(y_row[:, t * P:(t + 1) * P], pM[0:1, 0:P], ACT.Copy).then_inc(y_copied, 1)

            tower = {3: tower_transpose, 5: tower_1, 7: tower_2, 9: tower_3}
            next_group = [0]

            def rounds(upto):
                while next_group[0] < min(upto, len(GROUPS)):
                    round_k(next_group[0])
                    next_group[0] += 1

            rounds(2)
            double_quad(0)
            for t in range(tiles):
                for n in range(UNITS):
                    for q in quads_before(n):
                        round_quad(t, q)
                    if t == 0:
                        rounds(2 + n)
                    if t >= 1 and n in tower:
                        tower[n](t - 1)
            for n in sorted(tower):
                tower[n](tiles - 1)

        @block.vector
        def _(dve):
            def low_k(g):
                dve.wait_ge(k_rounded, g + 1)
                cols = group_cols(g)
                raw = room[:, g % K_SLOTS, 0:cols]
                nc.vector.tensor_tensor(raw, raw, k_high[:, g % 2, 0:cols].bitcast(F32), ALU.subtract
                                        ).then_inc(k_low, 1)

            quads_done = [0]

            def low_quad(t, q):
                dve.wait_ge(quad_high, quads_done[0] + 1)
                s = QUAD * q % SLOTS
                nc.vector.tensor_tensor(xl[:, s:s + QUAD, :], pT[:, :, :], xh[:, s:s + QUAD, :].bitcast(F32),
                                        ALU.subtract).then_inc(quad_low, 1)
                quads_done[0] += 1

            def multiply(t, n):
                u = ORDER[n]
                count = t * UNITS + n
                side, ks, js = u["side"], u["ks"], u["js"]
                cols = len(u["pairs"]) * E
                dve.wait_ge(v_ready, count + 1)
                if count >= P_SLOTS:
                    dve.wait_ge(sums, count - P_SLOTS + 1)
                x = emb[t % 2][:, 2 * side * ks[0]:2 * side * (ks[0] + len(ks)), :].rearrange(
                    "p (k s) e -> p k (s e)", k=len(ks))[:, :, 0:side * E]
                x = x.unsqueeze(2).broadcast_to([P, len(ks), len(js), side * E])
                shape = dict(k=len(ks), j=len(js))
                nc.vector.tensor_tensor(
                    prod[:, count % P_SLOTS, 0:cols].rearrange("p (k j c) -> p k j c", **shape),
                    v[count % V_SLOTS][:, 0:cols].rearrange("p (k j c) -> p k j c", **shape),
                    x, ALU.mult).then_inc(products, 1)

            def add_up(t, n):
                u = ORDER[n]
                count = t * UNITS + n
                pairs = len(u["pairs"])
                dve.wait_ge(products, count + 1)
                if n == 0 and t >= 2:
                    dve.wait_ge(z_turned, t - 1)
                nc.vector.tensor_reduce(
                    z[t % 2][:, u["at"]:u["at"] + pairs],
                    prod[:, count % P_SLOTS, 0:pairs * E].rearrange("p (a e) -> p a e", e=E),
                    AX_X, ALU.add).then_inc(sums, 1)

            next_group = [0]

            def lows(upto):
                while next_group[0] < min(upto, len(GROUPS)):
                    low_k(next_group[0])
                    next_group[0] += 1

            lows(2)
            before = None
            for t in range(tiles):
                for n in range(UNITS):
                    for q in quads_before(n):
                        low_quad(t, q)
                    if t == 0:
                        lows(2 + n)
                    multiply(t, n)
                    if before:
                        add_up(*before)
                    before = (t, n)
            add_up(*before)


def kernel(**inputs):
    import concourse.bacc as bacc
    from concourse.bass_utils import run_bass_kernel_spmd

    def chunks(a):
        a = np.asarray(a)
        return np.ascontiguousarray(a.reshape(a.shape[0] // P, P, -1).transpose(1, 0, 2))

    ids = np.asarray(inputs["ids"])
    tiles = ids.shape[0] // P
    k = np.asarray(inputs["L0_rec_kernel"])[:, STORED_TO_TRIU, :].reshape(E, PAIRS * E)
    halves = [[], []]
    for group in GROUPS:
        for u in group:
            n = len(u["pairs"]) * E // 2
            for half in range(2):
                at = u["at"] * E + half * n
                halves[half].append(k[:, at:at + n])
    k_raw = np.concatenate([np.concatenate(h, axis=1) for h in halves], axis=0)
    w1 = np.asarray(inputs["W_top1"])
    rows = np.concatenate([STORED_TO_TRIU, np.arange(PAIRS, w1.shape[0])])

    arrays = {
        "ids": np.ascontiguousarray(ids.reshape(tiles, P, FIELDS).transpose(1, 0, 2).reshape(P, -1)),
        "dense": np.asarray(inputs["dense_ctx"]),
        "k_raw": np.ascontiguousarray(k_raw),
        "w1": chunks(w1[rows]),
        "b1": np.ascontiguousarray(np.asarray(inputs["b_top1"]).reshape(-1, P).T),
        "w2": chunks(inputs["W_top2"]),
        "b2": np.ascontiguousarray(np.asarray(inputs["b_top2"]).reshape(-1, P).T),
        "w3": np.ascontiguousarray(np.asarray(inputs["W_top3"]).reshape(-1, P).T),
    }
    for f in range(FIELDS):
        arrays[f"tbl_{f}"] = np.asarray(inputs[f"tbl_{f}"])
    nc = bacc.Bacc("TRN2", target_bir_lowering=False, num_devices=1)
    dram = {n: nc.dram_tensor(n, a.shape, mybir.dt.from_np(a.dtype), kind="ExternalInput").ap()
            for n, a in arrays.items()}
    y = nc.dram_tensor("y", (1, tiles * P), F32, kind="ExternalOutput").ap()
    interaction_tower(nc, dram["ids"], dram["dense"], [dram[f"tbl_{f}"] for f in range(FIELDS)], dram["k_raw"],
                      dram["w1"], dram["b1"], dram["w2"], dram["b2"], dram["w3"], y)
    result = run_bass_kernel_spmd(nc, [arrays], core_ids=[0])
    return result.results[0]["y"].reshape(tiles * P, 1)
```

```python
from contextlib import ExitStack

import numpy as np

import concourse.bass as bass
from concourse import mybir
from concourse.alu_op_type import AluOpType as ALU

F32 = mybir.dt.float32
F32R = mybir.dt.float32r
I32 = mybir.dt.int32
ACT = mybir.ActivationFunctionType
AX_X = mybir.AxisListType.X

P = 128
FIELDS = 32
E = 64
PAIRS = FIELDS * (FIELDS - 1) // 2
UNIT = 16
QUAD = 4
SLOTS = 16
V_SLOTS = 3
P_SLOTS = 4
MORE_SLOTS = 3
PARTS = 8
K_SLOTS = 4
K_AHEAD = 3


def plan():
    def unit(side, ks, js):
        pairs = [(2 * side * k + i, 2 * side * k + side + j) for k in ks for j in js for i in range(side)]
        return dict(side=side, ks=list(ks), js=list(js), pairs=pairs)

    sq4 = [unit(4, [k], range(4)) for k in range(4)]
    sq8 = [[unit(8, [k], (2 * q, 2 * q + 1)) for q in range(4)] for k in range(2)]
    sq2 = [unit(2, range(4 * h, 4 * h + 4), range(2)) for h in range(2)]
    sq1 = [unit(1, range(8 * h, 8 * h + 8), range(1)) for h in range(2)]
    sq16 = [unit(16, [0], [j]) for j in range(16)]
    order = ([sq4[1], sq8[0][2], sq8[0][3], sq2[0], sq1[0], sq4[0], sq8[0][0], sq8[0][1]]
             + sq16[12:] + sq16[8:12] + [sq4[3], sq4[2], sq2[1], sq1[1]]
             + [sq8[1][2], sq8[1][3], sq8[1][0], sq8[1][1]] + sq16[4:8] + sq16[:4])
    full = [u for u in order if len(u["pairs"]) == UNIT]
    groups = [full[n:n + 2] for n in range(0, len(full), 2)]
    groups.insert(2, sq1)
    at = 0
    for g, group in enumerate(groups):
        for u in group:
            u["at"], u["group"] = at, g
            at += len(u["pairs"])
    assert at == PAIRS
    return order, groups


ORDER, GROUPS = plan()
UNITS = len(ORDER)
STORED = [pair for group in GROUPS for u in group for pair in u["pairs"]]
TRIU = {(i, j): i * (2 * FIELDS - i - 1) // 2 + j - i - 1 for i in range(FIELDS) for j in range(i + 1, FIELDS)}
STORED_TO_TRIU = np.array([TRIU[pair] for pair in STORED])
FIRST_USE = {q: min(n for n, u in enumerate(ORDER) if any(j // QUAD == q for _, j in u["pairs"])) for q in range(8)}
LAST_USE = {q: max(n for n, u in enumerate(ORDER) if any(j // QUAD == q for _, j in u["pairs"])) for q in range(8)}
QUADS = sorted(range(8), key=lambda q: (FIRST_USE[q], q))
GATHER_UNITS = 31
GATHER_ORDER = (3, 2, 1, 0, 7, 6, 5, 4)


QUAD_AT = {3: -7, 2: -5, 1: -2, 0: 0, 7: 5, 6: 8, 5: 11, 4: 13}
QUAD_FIRST = [0, 0, 1, 2]
PIECE_AT = [14, 16, 17, 18, 19, 21, 22, 23, 25, 29, 31]


def quad_schedule(tiles):
    at = {}
    for t in range(tiles):
        for q, n in QUAD_AT.items():
            c = t * UNITS + n if t or n > 0 else QUAD_FIRST[3 - q]
            assert c <= t * UNITS + FIRST_USE[q] - (3 if t else 0)
            if q >= 4 or t:
                assert c > (t if q >= 4 else t - 1) * UNITS + LAST_USE[(q + 4) % 8]
            at.setdefault(c, []).append((t, q))
    return at


TILE_0 = 'PDDP.APDGPGPDDPDGPA.PADPDGAPAPRR'
TILE_1 = 'PDGG.RPAPAGAGRGAGRA.RRPDPDDGRAPG'
TILE_2 = 'GGRA.PAGAPGADAGDGGR.DGPGGAGRAPGA'
TILE_3 = 'RGGA.PARAGGPAGGAGDA.RRPGRARPRPDG'


def shares(tiles):
    name = dict(P="pe", D="dve", G="pool", R="pool4", A="act")
    rows = [row.replace(".", "D") for row in (TILE_0, TILE_1, TILE_2, TILE_3)]
    assert len(rows) == tiles
    assert all(len(row) == UNITS for row in rows)
    return [name[a] for row in rows for a in row]


LAG = {'dve': 1, 'pe': 3, 'pool': 2, 'pool4': 4}
LEFT = {"pool": E // 2, "pool4": E // 4}
ACT_PAIRS = 6


def interaction_tower(nc, ids, dense, tables, k_raw, w1, b1, w2, b2, w3, y):
    tiles = dense.shape[0] // P
    zd = PAIRS + dense.shape[1]
    h1_dim, h2_dim = w1.shape[-1], w2.shape[-1]
    c0, c1, c2 = zd // P, h1_dim // P, h2_dim // P
    how = shares(tiles)

    def nth(kind, count):
        return how[:count + 1].count(kind)

    def tile_end(kind, t):
        return nth(kind, (t + 1) * UNITS - 1)

    pieces = [("turn", c) for c in range(c0)] + [("one", n) for n in range(c1)] + [("two", n) for n in range(c2)]
    pieces += [("three", 0)]
    ONE, TWO, THREE = c0, c0 + c1, c0 + c1 + c2
    quads_before = quad_schedule(tiles)
    quads = [tq for c in sorted(quads_before) for tq in quads_before[c]]
    pieces_after = {}
    for t in range(1, tiles):
        for i, n in enumerate(PIECE_AT):
            pieces_after.setdefault(t * UNITS + n, []).append((t - 1, i))

    with ExitStack() as ctx:
        def sb(name, shape, dt=F32):
            return ctx.enter_context(nc.sbuf_tensor(name, shape, dt))

        def psum(name, shape):
            return ctx.enter_context(nc.psum_tensor(name, shape, F32))

        def sem(name):
            return ctx.enter_context(nc.semaphore(name))

        kk = sb("kk", [P, PAIRS * E], F32R)
        emb = [sb(f"emb{i}", [P, FIELDS, E]) for i in range(2)]
        twice = sb("twice", [P, QUAD, 2, E])
        xh = sb("xh", [P, SLOTS, P], F32R)
        xl = sb("xl", [P, SLOTS, P], F32R)
        prod = sb("prod", [P, P_SLOTS, UNIT * E])
        room = sb("room", [P, K_SLOTS, UNIT * E])
        k_high = sb("k_high", [P, 2, UNIT * E])
        z = [sb(f"z{i}", [P, zd]) for i in range(2)]
        zT = sb("zT", [P, c0, P])
        h1T = sb("h1T", [P, c1, P])
        h2T = zT[:, 0:c2, :]
        y_sb = sb("y_sb", [1, P])
        idx = sb("idx", [P, tiles * FIELDS], I32)
        ident = sb("ident", [P, P])
        b1_sb = sb("b1_sb", [P, c1])
        b2_sb = sb("b2_sb", [P, c2])
        w3_sb = sb("w3_sb", [P, c2])
        flat_room = room[:, :, :].rearrange("p a b -> p (a b)")
        w1_sb = flat_room[:, 0:c0 * h1_dim].rearrange("p (c n) -> p c n", c=c0)
        w2_sb = flat_room[:, c0 * h1_dim:c0 * h1_dim + c1 * h2_dim].rearrange("p (c n) -> p c n", c=c1)

        v = [psum(f"v{i}", [P, UNIT * E]) for i in range(V_SLOTS)]
        pT = psum("pT", [P, QUAD, P])
        partial = psum("partial", [P, 4 * P])

        ids_in = sem("ids_in")
        ident_zero, ident_ready = sem("ident_zero"), sem("ident_ready")
        gathered = [[sem(f"gathered{h}_{q}") for q in range(FIELDS // QUAD)] for h in range(2)]
        k_in = [sem(f"k_in{i}") for i in range(K_SLOTS)]
        k_rounded = sem("k_rounded")
        k_placed = [sem(f"k_placed{i}") for i in range(2)]
        k_low = sem("k_low")
        k_moved = [sem(f"k_moved{i}") for i in range(K_SLOTS)]
        small_in = sem("small_in")
        w_in = sem("w_in")
        dense_in = [sem(f"dense_in{i}") for i in range(2)]
        quad_doubled, quad_transposed = sem("quad_doubled"), sem("quad_transposed")
        quad_high, quad_low = sem("quad_high"), sem("quad_low")
        v_ready = sem("v_ready")
        products = sem("products")
        partly = {kind: sem(f"partly_{kind}") for kind in ("pe", "pool", "pool4")}
        halved = sem("halved")
        kinds = ("dve", "pe", "pool", "pool4", "act")
        summed = {kind: sem(f"summed_{kind}") for kind in kinds}
        piece_made, piece_taken = sem("piece_made"), sem("piece_taken")
        y_out = sem("y_out")

        def group_cols(g):
            return sum(len(u["pairs"]) for u in GROUPS[g]) * E // 2

        def placed(g, half, side):
            n = len(GROUPS[g][0]["pairs"]) * E
            at = GROUPS[g][0]["at"] * E
            both = kk[64 * side:64 * side + 64, at:at + 2 * n].rearrange("p (u h c) -> p u h c", u=2, h=2)
            return both[:, :, half, :]

        def packed(buf, g, half):
            return buf[64 * half:64 * half + 64, 0:group_cols(g)].rearrange("p (u c) -> p u c", u=2)


        def ring(t):
            return [prod[:, i, :] for i in range(P_SLOTS)] + (
                [k_high[:, 0, :], k_high[:, 1, :], room[:, K_SLOTS - 1, :]] if t >= 1 else [])

        slot_of, last_in = [], []
        taken = {}
        for c in range(tiles * UNITS):
            n = len(ring(c // UNITS))
            slot_of.append(c % n)
            last_in.append(taken.get(c % n))
            taken[c % n] = c

        def products_of(c):
            return ring(c // UNITS)[slot_of[c]]

        def wait_slot(eng, c):
            b = last_in[c]
            if b is not None:
                done = partly["pe"] if how[b] == "pe" else summed[how[b]]
                eng.wait_ge(done, nth(how[b], b))

        def wait_z(eng, t):
            for kind in kinds:
                if tile_end(kind, t):
                    eng.wait_ge(summed[kind], tile_end(kind, t))

        def piece_out(t, i):
            return pT[:, 0, :] if t < tiles - 1 else v[i % V_SLOTS][:, 0:P]

        def wait_z_free(eng, t):
            if t >= 2:
                eng.wait_ge(piece_made, (t - 2) * len(pieces) + c0)

        block = ctx.enter_context(nc.Block())

        @block.sync
        def _(sp):
            sp.dma_start(idx[:, :], ids).then_inc(ids_in, 16)

            def load_k(g):
                cols = group_cols(g)
                at = GROUPS[g][0]["at"] * E // 2
                sp.dma_start(room[:, g % K_SLOTS, 0:cols], k_raw[:, at:at + cols]).then_inc(k_in[g % K_SLOTS], 16)

            def load_dense(t):
                sp.dma_start(z[t % 2][:, PAIRS:zd], dense[t * P:(t + 1) * P, :]).then_inc(dense_in[t % 2], 16)

            for g in range(K_SLOTS):
                load_k(g)
            for g in range(len(GROUPS)):
                sp.wait_ge(k_rounded, g + 1)
                for half in range(2):
                    sp.dma_start(placed(g, half, half).bitcast(F32), packed(k_high[:, g % 2, :], g, half)
                                 ).then_inc(k_placed[g % 2], 16)
                sp.wait_ge(k_low, g + 1)
                for half in range(2):
                    sp.dma_start(placed(g, half, 1 - half).bitcast(F32), packed(room[:, g % K_SLOTS, :], g, half)
                                 ).then_inc(k_moved[g % K_SLOTS], 16)
                if g >= 1 and g - 1 + K_SLOTS < len(GROUPS):
                    sp.wait_ge(k_moved[(g - 1) % K_SLOTS], 32 * ((g - 1) // K_SLOTS + 1))
                    load_k(g - 1 + K_SLOTS)
            for t in range(2):
                load_dense(t)
            for s in range(K_SLOTS):
                sp.wait_ge(k_moved[s], 32 * len(range(s, len(GROUPS), K_SLOTS)))
            sp.dma_start(b1_sb[:, :], b1).then_inc(small_in, 16)
            sp.dma_start(b2_sb[:, :], b2).then_inc(small_in, 16)
            sp.dma_start(w3_sb[:, :], w3).then_inc(small_in, 16)
            sp.dma_start(w1_sb, w1).then_inc(w_in, 16)
            sp.dma_start(w2_sb, w2).then_inc(w_in, 16)
            for t in range(tiles):
                if t >= 2:
                    wait_z_free(sp, t)
                    load_dense(t)
                sp.wait_ge(piece_taken, (t + 1) * len(pieces))
                sp.dma_start(y[:, t * P:(t + 1) * P], y_sb[:, :]).then_inc(y_out, 16)
            sp.wait_ge(y_out, 16 * tiles)

        @block.gpsimd
        def _(pool):
            nc.gpsimd.memset(ident[:, :], 0.0).then_inc(ident_zero, 1)
            pool.wait_ge(ident_zero, 1)
            nc.gpsimd.affine_select(out=ident[:, :], in_=ident[:, :], pattern=[[-1, P]], compare_op=ALU.not_equal,
                                    fill=1.0, base=0, channel_multiplier=1).then_inc(ident_ready, 1)
            pool.wait_ge(ids_in, 16)

            def gather(t, fields):
                for f in fields:
                    c = t * FIELDS + f
                    nc.gpsimd.indirect_dma_start(
                        emb[t % 2][:, f, :], None, tables[f],
                        bass.IndirectOffsetOnAxis(idx[:, c:c + 1], 0)).then_inc(gathered[t % 2][f // QUAD], 16)

            def fold(c):
                pool.wait_ge(products, c + 1)
                x = products_of(c).rearrange("p (a e) -> p a e", e=E)
                half, quarter = E // 2, E // 4
                once = nc.gpsimd.tensor_tensor(x[:, :, 0:half], x[:, :, 0:half], x[:, :, half:E], ALU.add)
                if how[c] == "pool":
                    once.then_inc(partly["pool"], 1)
                else:
                    once.then_inc(halved, 1)
                    pool.wait_ge(halved, nth("pool4", c))
                    nc.gpsimd.tensor_tensor(x[:, :, 0:quarter], x[:, :, 0:quarter], x[:, :, quarter:half], ALU.add
                                            ).then_inc(partly["pool4"], 1)

            fields = [f for q in GATHER_ORDER for f in range(QUAD * q, QUAD * q + QUAD)]
            gather(0, fields)
            for t in range(tiles):
                if 1 <= t < tiles - 1:
                    pool.wait_ge(products, t * UNITS)
                for n in range(UNITS):
                    if how[t * UNITS + n] in LEFT:
                        fold(t * UNITS + n)
                    if t < tiles - 1:
                        gather(t + 1, fields[FIELDS * n // GATHER_UNITS:FIELDS * (n + 1) // GATHER_UNITS])

        @block.tensor
        def _(pe):
            pe.wait_ge(ident_ready, 1)
            quads_done, pieces_done = [0], [0]

            def transpose_quad():
                pe.wait_ge(quad_doubled, quads_done[0] + 1)
                pe.wait_ge(quad_low, quads_done[0])
                if pieces_done[0]:
                    pe.wait_ge(piece_taken, pieces_done[0])
                for r in range(QUAD):
                    x = twice[:, r, :, :].rearrange("p a e -> p (a e)")
                    last = nc.tensor.transpose(pT[:, r, :], x, ident[:, :])
                last.then_inc(quad_transposed, 1)
                quads_done[0] += 1
                return quads_done[0]

            def unit(t, n, split_count):
                u = ORDER[n]
                count = t * UNITS + n
                if t == 0:
                    g = u["group"]
                    pe.wait_ge(k_placed[g % 2], 32 * (g // 2 + 1))
                    pe.wait_ge(k_moved[g % K_SLOTS], 32 * (g // K_SLOTS + 1))
                pe.wait_ge(quad_low, split_count)
                if count >= V_SLOTS:
                    pe.wait_ge(products, count - V_SLOTS + 1)
                out, at = v[count % V_SLOTS], u["at"] * E
                side, pos = u["side"], 0
                for k in u["ks"]:
                    for j in u["js"]:
                        slot = (2 * side * k + side + j) % SLOTS
                        width = side * E
                        pieces = [(pos + o, min(512, width)) for o in range(0, width, 512)]
                        for part in (xh, xl):
                            for o, w in pieces:
                                last = nc.tensor.matmul(out[:, o:o + w], part[:, slot, :], kk[:, at + o:at + o + w],
                                                        start=part is xh, stop=part is xl)
                        pos += width
                last.then_inc(v_ready, 1)

            def sum_parts(c):
                pe.wait_ge(products, c + 1)
                order = nth("pe", c)
                if order > 1:
                    pe.wait_ge(summed["pe"], order - 1)
                x = products_of(c).rearrange("p (a g s) -> p a g s", g=E // PARTS, s=PARTS)
                out = partial[:, 0:UNIT * PARTS].rearrange("p (a s) -> p a s", s=PARTS)
                for g in range(E // PARTS):
                    last = nc.tensor.matmul(out, ident[:, :], x[:, :, g, :], start=g == 0, stop=g == E // PARTS - 1)
                last.then_inc(partly["pe"], 1)

            def layer_chunk(out, w, x, chunks, n, width=P):
                for c in range(chunks):
                    last = nc.tensor.matmul(out, w[:, c, n * width:(n + 1) * width], x[:, c, :],
                                            start=c == 0, stop=c == chunks - 1)
                return last

            def piece(t, i):
                kind, n = pieces[i]
                count = t * len(pieces) + i
                base = t * len(pieces)
                out = piece_out(t, i)
                if t < tiles - 1:
                    pe.wait_ge(quad_low, quads_done[0])
                    if count:
                        pe.wait_ge(piece_taken, count)
                elif i >= V_SLOTS:
                    pe.wait_ge(piece_taken, count - V_SLOTS + 1)
                pieces_done[0] = count + 1
                if i == 0:
                    wait_z(pe, t)
                    pe.wait_ge(dense_in[t % 2], 16 * (t // 2 + 1))
                if i == ONE and t == 0:
                    pe.wait_ge(w_in, 32)
                    pe.wait_ge(small_in, 48)
                if i in (ONE, TWO, THREE):
                    pe.wait_ge(piece_taken, base + i)
                if kind == "turn":
                    last = nc.tensor.transpose(out, z[t % 2][:, n * P:(n + 1) * P], ident[:, :])
                elif kind == "one":
                    last = layer_chunk(out, w1_sb, zT, c0, n)
                elif kind == "two":
                    last = layer_chunk(out, w2_sb, h1T, c1, n)
                else:
                    last = layer_chunk(out[0:1, :], w3_sb[:, :].unsqueeze(2), h2T, c2, 0, 1)
                last.then_inc(piece_made, 1)

            split_at = {}
            for t in range(tiles):
                for n in range(UNITS):
                    c = t * UNITS + n
                    for quad in quads_before.get(c, []):
                        split_at[quad] = transpose_quad()
                    to_sum = c >= V_SLOTS and how[c - V_SLOTS] == "pe"
                    if to_sum and t == 0:
                        sum_parts(c - V_SLOTS)
                    unit(t, n, max(split_at[t, j // QUAD] for _, j in ORDER[n]["pairs"]))
                    if to_sum and t >= 1:
                        sum_parts(c - V_SLOTS)
                    for p in pieces_after.get(c, []):
                        piece(*p)
            for c in range(tiles * UNITS - V_SLOTS, tiles * UNITS):
                if how[c] == "pe":
                    sum_parts(c)
            for i in range(len(pieces)):
                piece(tiles - 1, i)

        @block.scalar
        def _(act):
            def round_k(g):
                act.wait_ge(k_in[g % K_SLOTS], 16 * (g // K_SLOTS + 1))
                if g >= 2:
                    act.wait_ge(k_low, g - 1)
                    act.wait_ge(k_placed[g % 2], 32 * (g // 2))
                cols = group_cols(g)
                nc.scalar.activation(k_high[:, g % 2, 0:cols].bitcast(F32R), room[:, g % K_SLOTS, 0:cols], ACT.Copy
                                     ).then_inc(k_rounded, 1)

            def double_quad(i):
                t, q = quads[i]
                act.wait_ge(gathered[t % 2][q], 16 * QUAD * (t // 2 + 1))
                act.wait_ge(quad_transposed, i)
                x = emb[t % 2][:, QUAD * q:QUAD * q + QUAD, :].unsqueeze(2).broadcast_to([P, QUAD, 2, E])
                nc.scalar.activation(twice[:, :, :, :], x, ACT.Copy).then_inc(quad_doubled, 1)

            quads_done = [0]

            def round_quad(t, q):
                if quads_done[0] + 1 < len(quads):
                    double_quad(quads_done[0] + 1)
                act.wait_ge(quad_transposed, quads_done[0] + 1)
                done = (t - 1) * UNITS + LAST_USE[q + 4] + 1 if q < 4 else t * UNITS + LAST_USE[q - 4] + 1
                if done > 0:
                    act.wait_ge(v_ready, done)
                s = QUAD * q % SLOTS
                nc.scalar.activation(xh[:, s:s + QUAD, :], pT[:, :, :], ACT.Copy).then_inc(quad_high, 1)
                quads_done[0] += 1

            to_sum = []

            def sum_up(most):
                for c, a in to_sum[:most]:
                    u = ORDER[c % UNITS]
                    if a == 0:
                        act.wait_ge(products, c + 1)
                        wait_z_free(act, c // UNITS)
                    e = products_of(c)[:, a * E:(a + 1) * E]
                    at = u["at"] + a
                    last = nc.scalar.activation(e, e, ACT.Copy, accum_out=z[c // UNITS % 2][:, at:at + 1])
                    if a == UNIT - 1:
                        last.then_inc(summed["act"], 1)
                del to_sum[:most]

            def take_piece(t, i):
                kind, n = pieces[i]
                count = t * len(pieces) + i
                x = piece_out(t, i)
                if count == 0:
                    act.wait_ge(small_in, 48)
                act.wait_ge(piece_made, count + 1)
                if kind == "turn":
                    last = nc.scalar.activation(zT[:, n, :], x, ACT.Copy)
                elif kind == "one":
                    last = nc.scalar.activation(h1T[:, n, :], x, ACT.Relu, bias=b1_sb[:, n:n + 1])
                elif kind == "two":
                    last = nc.scalar.activation(h2T[:, n, :], x, ACT.Relu, bias=b2_sb[:, n:n + 1])
                else:
                    if t >= 1:
                        act.wait_ge(y_out, 16 * t)
                    last = nc.scalar.activation(y_sb[:, :], x[0:1, :], ACT.Copy)
                last.then_inc(piece_taken, 1)

            next_group = [0]

            def rounds(upto):
                while next_group[0] < min(upto, len(GROUPS)):
                    round_k(next_group[0])
                    next_group[0] += 1

            rounds(K_AHEAD)
            double_quad(0)
            for t in range(tiles):
                for n in range(UNITS):
                    c = t * UNITS + n
                    for quad in quads_before.get(c, []):
                        round_quad(*quad)
                    if t == 0:
                        rounds(ORDER[n]["group"] + 1 + K_AHEAD)
                    for p in pieces_after.get(c, []):
                        take_piece(*p)
                    if c >= V_SLOTS and how[c - V_SLOTS] == "act":
                        to_sum.extend((c - V_SLOTS, a) for a in range(UNIT))
                    sum_up(ACT_PAIRS)
            for c in range(tiles * UNITS - V_SLOTS, tiles * UNITS):
                if how[c] == "act":
                    to_sum.extend((c, a) for a in range(UNIT))
            sum_up(len(to_sum))
            for i in range(len(pieces)):
                take_piece(tiles - 1, i)

        @block.vector
        def _(dve):
            def low_k(g):
                dve.wait_ge(k_rounded, g + 1)
                cols = group_cols(g)
                raw = room[:, g % K_SLOTS, 0:cols]
                nc.vector.tensor_tensor(raw, raw, k_high[:, g % 2, 0:cols], ALU.subtract
                                        ).then_inc(k_low, 1)

            quads_done = [0]

            def low_quad(t, q):
                dve.wait_ge(quad_high, quads_done[0] + 1)
                s = QUAD * q % SLOTS
                nc.vector.tensor_tensor(xl[:, s:s + QUAD, :], pT[:, :, :], xh[:, s:s + QUAD, :].bitcast(F32),
                                        ALU.subtract).then_inc(quad_low, 1)
                quads_done[0] += 1

            seen = [set() for _ in range(tiles)]

            def multiply(t, n):
                u = ORDER[n]
                count = t * UNITS + n
                side, ks, js = u["side"], u["ks"], u["js"]
                cols = len(u["pairs"]) * E
                dve.wait_ge(v_ready, count + 1)
                if t == 1 and n == 0:
                    for s in range(2):
                        dve.wait_ge(k_placed[s], 32 * len(range(s, len(GROUPS), 2)))
                    last_slot = K_SLOTS - 1
                    dve.wait_ge(k_moved[last_slot], 32 * len(range(last_slot, len(GROUPS), K_SLOTS)))
                wait_slot(dve, count)
                for q in sorted({i // QUAD for i, _ in u["pairs"]} - seen[t]):
                    dve.wait_ge(gathered[t % 2][q], 16 * QUAD * (t // 2 + 1))
                    seen[t].add(q)
                x = emb[t % 2][:, 2 * side * ks[0]:2 * side * (ks[0] + len(ks)), :].rearrange(
                    "p (k s) e -> p k (s e)", k=len(ks))[:, :, 0:side * E]
                x = x.unsqueeze(2).broadcast_to([P, len(ks), len(js), side * E])
                shape = dict(k=len(ks), j=len(js))
                nc.vector.tensor_tensor(
                    products_of(count)[:, 0:cols].rearrange("p (k j c) -> p k j c", **shape),
                    v[count % V_SLOTS][:, 0:cols].rearrange("p (k j c) -> p k j c", **shape),
                    x, ALU.mult).then_inc(products, 1)

            def finish(c):
                u, kind = ORDER[c % UNITS], how[c]
                pairs = len(u["pairs"])
                if kind == "dve":
                    dve.wait_ge(products, c + 1)
                    x = products_of(c)[:, 0:pairs * E].rearrange("p (a e) -> p a e", e=E)
                else:
                    dve.wait_ge(partly[kind], nth(kind, c))
                    if kind in LEFT:
                        x = products_of(c).rearrange("p (a e) -> p a e", e=E)[:, :, 0:LEFT[kind]]
                    else:
                        x = partial[:, 0:UNIT * PARTS].rearrange("p (a s) -> p a s", s=PARTS)
                nc.vector.tensor_reduce(z[c // UNITS % 2][:, u["at"]:u["at"] + pairs], x, AX_X, ALU.add
                                        ).then_inc(summed[kind], 1)

            next_group = [0]

            def lows(upto):
                while next_group[0] < min(upto, len(GROUPS)):
                    low_k(next_group[0])
                    next_group[0] += 1

            lows(K_AHEAD)
            units = tiles * UNITS
            for c in range(units + max(LAG.values())):
                t, n = divmod(c, UNITS)
                for quad in quads_before.get(c, []):
                    low_quad(*quad)
                if c < units:
                    if t == 0:
                        lows(ORDER[n]["group"] + 1 + K_AHEAD)
                    multiply(t, n)
                for kind, lag in LAG.items():
                    if lag <= c < units + lag and how[c - lag] == kind:
                        if (c - lag) % UNITS == 0:
                            wait_z_free(dve, (c - lag) // UNITS)
                        finish(c - lag)


def kernel(**inputs):
    import concourse.bacc as bacc
    from concourse.bass_utils import run_bass_kernel_spmd

    def chunks(a):
        a = np.asarray(a)
        return np.ascontiguousarray(a.reshape(a.shape[0] // P, P, -1).transpose(1, 0, 2))

    ids = np.asarray(inputs["ids"])
    tiles = ids.shape[0] // P
    k = np.asarray(inputs["L0_rec_kernel"])[:, STORED_TO_TRIU, :].reshape(E, PAIRS * E)
    halves = [[], []]
    for group in GROUPS:
        for u in group:
            n = len(u["pairs"]) * E // 2
            for half in range(2):
                at = u["at"] * E + half * n
                halves[half].append(k[:, at:at + n])
    k_raw = np.concatenate([np.concatenate(h, axis=1) for h in halves], axis=0)
    w1 = np.asarray(inputs["W_top1"])
    rows = np.concatenate([STORED_TO_TRIU, np.arange(PAIRS, w1.shape[0])])

    arrays = {
        "ids": np.ascontiguousarray(ids.reshape(tiles, P, FIELDS).transpose(1, 0, 2).reshape(P, -1)),
        "dense": np.asarray(inputs["dense_ctx"]),
        "k_raw": np.ascontiguousarray(k_raw),
        "w1": chunks(w1[rows]),
        "b1": np.ascontiguousarray(np.asarray(inputs["b_top1"]).reshape(-1, P).T),
        "w2": chunks(inputs["W_top2"]),
        "b2": np.ascontiguousarray(np.asarray(inputs["b_top2"]).reshape(-1, P).T),
        "w3": np.ascontiguousarray(np.asarray(inputs["W_top3"]).reshape(-1, P).T),
    }
    for f in range(FIELDS):
        arrays[f"tbl_{f}"] = np.asarray(inputs[f"tbl_{f}"])
    nc = bacc.Bacc("TRN2", target_bir_lowering=False, num_devices=1)
    dram = {n: nc.dram_tensor(n, a.shape, mybir.dt.from_np(a.dtype), kind="ExternalInput").ap()
            for n, a in arrays.items()}
    y = nc.dram_tensor("y", (1, tiles * P), F32, kind="ExternalOutput").ap()
    interaction_tower(nc, dram["ids"], dram["dense"], [dram[f"tbl_{f}"] for f in range(FIELDS)], dram["k_raw"],
                      dram["w1"], dram["b1"], dram["w2"], dram["b2"], dram["w3"], y)
    result = run_bass_kernel_spmd(nc, [arrays], core_ids=[0])
    return result.results[0]["y"].reshape(tiles * P, 1)
```

```python
from contextlib import ExitStack

import numpy as np

import concourse.bass as bass
from concourse import mybir
from concourse.alu_op_type import AluOpType as ALU

F32 = mybir.dt.float32
F32R = mybir.dt.float32r
I32 = mybir.dt.int32
ACT = mybir.ActivationFunctionType
AX_X = mybir.AxisListType.X

P = 128
FIELDS = 32
E = 64
PAIRS = FIELDS * (FIELDS - 1) // 2
UNIT = 16
QUAD = 4
SLOTS = 16
V_SLOTS = 3
P_SLOTS = 4
PARTS = 8
LEFT = {"pool": E // 2, "pool4": E // 4}
K_SLOTS = 4


def plan():
    def unit(side, ks, js):
        pairs = [(2 * side * k + i, 2 * side * k + side + j) for k in ks for j in js for i in range(side)]
        return dict(side=side, ks=list(ks), js=list(js), pairs=pairs)

    def quarter(i0, j0):
        return dict(side=4, ks=[0], js=list(range(4)), pairs=[(i0 + i, j0 + j) for j in range(4) for i in range(4)])

    sq4 = [unit(4, [k], range(4)) for k in range(4)]
    sq8 = [unit(8, [1], (2 * q, 2 * q + 1)) for q in range(4)]
    sq2 = [unit(2, range(4 * h, 4 * h + 4), range(2)) for h in range(2)]
    sq1 = [unit(1, range(8 * h, 8 * h + 8), range(1)) for h in range(2)]
    sq16 = [unit(16, [0], [j]) for j in range(16)]
    order = ([sq4[1], quarter(4, 12), quarter(4, 8), quarter(0, 12), sq2[0], sq1[0], sq4[0], quarter(0, 8)]
             + sq16[12:] + sq16[8:12] + [sq4[3], sq4[2], sq2[1], sq1[1]]
             + [sq8[2], sq8[3], sq8[0], sq8[1]] + sq16[4:8] + sq16[:4])
    full = [u for u in order if len(u["pairs"]) == UNIT]
    groups = [full[n:n + 2] for n in range(0, len(full), 2)]
    groups.insert(2, sq1)
    at = 0
    for g, group in enumerate(groups):
        for u in group:
            u["at"], u["group"] = at, g
            at += len(u["pairs"])
    assert at == PAIRS
    return order, groups


ORDER, GROUPS = plan()
UNITS = len(ORDER)
STORED = [pair for group in GROUPS for u in group for pair in u["pairs"]]
TRIU = {(i, j): i * (2 * FIELDS - i - 1) // 2 + j - i - 1 for i in range(FIELDS) for j in range(i + 1, FIELDS)}
STORED_TO_TRIU = np.array([TRIU[pair] for pair in STORED])
FIRST_USE = {q: min(n for n, u in enumerate(ORDER) if any(j // QUAD == q for _, j in u["pairs"])) for q in range(8)}
LAST_USE = {q: max(n for n, u in enumerate(ORDER) if any(j // QUAD == q for _, j in u["pairs"])) for q in range(8)}
GATHER_ORDER = (3, 2, 1, 0, 7, 6, 5, 4)


TILE_0 = 'PDADP.GPRGGPRGGPRPA.RAGPARDPRDAP'
TILE_1 = 'DRGGD.PAGPADGGDGAGA.DRDGGGGDRGPA'
TILE_2 = 'DAGDP.GGGAAPARDADRD.GGGADGRDGAPA'
TILE_3 = 'GRGRG.ARRGRGPRRGAGA.RRRAARAPDGRG'
LAG = {'dve': 2, 'pe': 3, 'pool': 3, 'pool4': 3}
PE_GROUPS = 4
ACT_PAIRS = 6
ACT_LAG = 3
QUAD_AT = {3: -7, 2: -4, 1: -2, 0: 0, 7: 6, 6: 8, 5: 10, 4: 14}
QUAD_FIRST = [0, 1, 1, 3]
DOUBLE_AHEAD = 5
SPLIT_AFTER = 0
PIECE_AT = [12, 15, 16, 18, 19, 20, 21, 23, 26, 27, 29]
K_AT = [-1, -1, 0, 0, 1, 4, 5, 7, 8, 10, 11, 12, 14, 15, 17, 23]
LOW_AT = [-1, -1, -1, 0, 1, 3, 4, 6, 8, 11, 13, 13, 16, 19, 20, 24]
BY_ACT = [1, 0, 0, 0, 0, 2, 0, 1, 0, 2, 1, 2, 0, 1, 0, 0]
GATHER_UNITS = 31


def quad_schedule(tiles):
    at = {}
    for t in range(tiles):
        for q, n in QUAD_AT.items():
            c = t * UNITS + n if t or n > 0 else QUAD_FIRST[3 - q]
            assert c <= t * UNITS + FIRST_USE[q] - (2 if t else 0)
            if q >= 4 or t:
                assert c > (t if q >= 4 else t - 1) * UNITS + LAST_USE[(q + 4) % 8]
            at.setdefault(c, []).append((t, q))
    return at


def pt_schedule(quads_before, pieces_after, units):
    before, after, pending = [[] for _ in range(units)], [[] for _ in range(units)], None
    for c in range(units):
        for quad in quads_before.get(c, []):
            if pending:
                before[c].append(("split", pending[0]))
            before[c].append(("turn", quad))
            pending = (quad, c)
            if c <= 3:
                before[c].append(("split", quad))
                pending = None
        here = pieces_after.get(c, [])
        if pending and (here or c >= pending[1] + SPLIT_AFTER):
            after[c].append(("split", pending[0]))
            pending = None
        after[c] += [("piece", p) for p in here]
    return before, after


def shares(tiles):
    name = dict(P="pe", D="dve", G="pool", R="pool4", A="act")
    rows = [row.replace(".", "D") for row in (TILE_0, TILE_1, TILE_2, TILE_3)]
    assert len(rows) == tiles
    assert all(len(row) == UNITS for row in rows)
    return [name[a] for row in rows for a in row]


def interaction_tower(nc, ids, dense, tables, k_raw, w1, b1, w2, b2, w3, y):
    tiles = dense.shape[0] // P
    zd = PAIRS + dense.shape[1]
    h1_dim, h2_dim = w1.shape[-1], w2.shape[-1]
    c0, c1, c2 = zd // P, h1_dim // P, h2_dim // P
    how = shares(tiles)

    def nth(kind, count):
        return how[:count + 1].count(kind)

    def tile_end(kind, t):
        return nth(kind, (t + 1) * UNITS - 1)

    pieces = [("turn", c) for c in range(c0)] + [("one", n) for n in range(c1)] + [("two", n) for n in range(c2)]
    pieces += [("three", 0)]
    ONE, TWO, THREE = c0, c0 + c1, c0 + c1 + c2
    quads_before = quad_schedule(tiles)
    quads = [tq for c in sorted(quads_before) for tq in quads_before[c]]
    unit_of = [c for c in sorted(quads_before) for _ in quads_before[c]]
    pieces_after = {}
    for t in range(1, tiles):
        for i, n in enumerate(PIECE_AT):
            pieces_after.setdefault(t * UNITS + n, []).append((t - 1, i))
    pt_before, pt_after = pt_schedule(quads_before, pieces_after, tiles * UNITS)

    with ExitStack() as ctx:
        def sb(name, shape, dt=F32):
            return ctx.enter_context(nc.sbuf_tensor(name, shape, dt))

        def psum(name, shape):
            return ctx.enter_context(nc.psum_tensor(name, shape, F32))

        def sem(name):
            return ctx.enter_context(nc.semaphore(name))

        kk = sb("kk", [P, PAIRS * E], F32R)
        emb = [sb(f"emb{i}", [P, FIELDS, E]) for i in range(2)]
        twice = sb("twice", [P, QUAD, 2, E])
        xh = sb("xh", [P, SLOTS, P], F32R)
        xl = sb("xl", [P, SLOTS, P], F32R)
        prod = sb("prod", [P, P_SLOTS, UNIT * E])
        room = sb("room", [P, K_SLOTS, UNIT * E])
        k_high = sb("k_high", [P, 2, UNIT * E])
        z = [sb(f"z{i}", [P, zd]) for i in range(2)]
        turned = sb("turned", [P, c0 + c1, P])
        zT, h1T = turned[:, 0:c0, :], turned[:, c0:c0 + c1, :]
        h2T = zT[:, 0:c2, :]
        y_row = h1T[0:1, 0, :]
        idx = sb("idx", [P, tiles * FIELDS], I32)
        ident = sb("ident", [P, P])
        minus_ident = sb("minus_ident", [P, P], F32R)
        b1_sb = sb("b1_sb", [P, c1])
        b2_sb = sb("b2_sb", [P, c2])
        w3_sb = sb("w3_sb", [P, c2])
        flat_room = room[:, :, :].rearrange("p a b -> p (a b)")
        w1_sb = flat_room[:, 0:c0 * h1_dim].rearrange("p (c n) -> p c n", c=c0)
        w2_sb = flat_room[:, c0 * h1_dim:c0 * h1_dim + c1 * h2_dim].rearrange("p (c n) -> p c n", c=c1)

        v = [psum(f"v{i}", [P, UNIT * E]) for i in range(V_SLOTS)]
        pT = psum("pT", [P, QUAD, P])
        partial = psum("partial", [P, 4 * P])

        ids_in = sem("ids_in")
        ident_zero, ident_ready, minus_ready = sem("ident_zero"), sem("ident_ready"), sem("minus_ready")
        gathered = [[sem(f"gathered{h}_{q}") for q in range(FIELDS // QUAD)] for h in range(2)]
        k_in = [sem(f"k_in{i}") for i in range(K_SLOTS)]
        k_rounded = sem("k_rounded")
        k_placed = [sem(f"k_placed{i}") for i in range(2)]
        k_low = sem("k_low")
        k_moved = [sem(f"k_moved{i}") for i in range(K_SLOTS)]
        small_in = sem("small_in")
        w_in = sem("w_in")
        dense_in = [sem(f"dense_in{i}") for i in range(2)]
        quad_doubled, quad_transposed = sem("quad_doubled"), sem("quad_transposed")
        quad_high, quad_left, quad_low = sem("quad_high"), sem("quad_left"), sem("quad_low")
        v_ready = sem("v_ready")
        products = sem("products")
        partly = {kind: sem(f"partly_{kind}") for kind in ("pe", "pool", "pool4")}
        halved = sem("halved")
        kinds = ("dve", "pe", "pool", "pool4", "act")
        summed = {kind: sem(f"summed_{kind}") for kind in kinds}
        piece_made, piece_taken = sem("piece_made"), sem("piece_taken")
        tail_made, tail_taken = sem("tail_made"), sem("tail_taken")
        y_out = sem("y_out")

        def group_cols(g):
            return len(GROUPS[g][0]["pairs"]) * E

        def placed(g, half, side):
            at = GROUPS[g][half]["at"] * E
            return kk[64 * side:64 * side + 64, at:at + group_cols(g)]

        def packed(buf, g, half):
            return buf[64 * half:64 * half + 64, 0:group_cols(g)]

        def ring(t):
            return [prod[:, i, :] for i in range(P_SLOTS)] + (
                [k_high[:, 0, :], k_high[:, 1, :], room[:, K_SLOTS - 1, :]] if t >= 1
                else [turned[:, :, :].rearrange("p c b -> p (c b)")[:, 0:UNIT * E]])

        slot_of, last_in = [], []
        taken = {}
        for c in range(tiles * UNITS):
            n = len(ring(c // UNITS))
            slot_of.append(c % n)
            last_in.append(taken.get(c % n))
            taken[c % n] = c

        def products_of(c):
            return ring(c // UNITS)[slot_of[c]]

        def wait_slot(eng, c):
            b = last_in[c]
            if b is not None:
                done = partly["pe"] if how[b] == "pe" else summed[how[b]]
                eng.wait_ge(done, nth(how[b], b))

        def wait_z(eng, t):
            for kind in kinds:
                if tile_end(kind, t):
                    eng.wait_ge(summed[kind], tile_end(kind, t))

        EARLY_TURNS, LAST_TURN, TAIL_ONE = 1, 2, 3
        TAIL_TWO = TAIL_ONE + c1
        TAIL_THREE = TAIL_TWO + c2
        early = c0 - 1
        early_unit = max(n for n, u in enumerate(ORDER) if u["at"] < early * P)
        early_slot = (tiles * UNITS - V_SLOTS) % V_SLOTS
        one_out = v[early_slot][:, 0:c1 * P].rearrange("p (n b) -> p n b", n=c1)
        two_out = [v[(early_slot + 1 + n) % V_SLOTS][:, 0:P] for n in range(c2)]

        def wait_z_free(eng, t):
            if t >= 2:
                eng.wait_ge(piece_made, (t - 2) * len(pieces) + c0)

        block = ctx.enter_context(nc.Block())

        @block.sync
        def _(sp):
            sp.dma_start(idx[:, :], ids).then_inc(ids_in, 16)

            def load_k(g):
                cols = group_cols(g)
                at = GROUPS[g][0]["at"] * E // 2
                sp.dma_start(room[:, g % K_SLOTS, 0:cols], k_raw[:, at:at + cols]).then_inc(k_in[g % K_SLOTS], 16)

            def load_dense(t):
                sp.dma_start(z[t % 2][:, PAIRS:zd], dense[t * P:(t + 1) * P, :]).then_inc(dense_in[t % 2], 16)

            for g in range(K_SLOTS):
                load_k(g)
            for g in range(len(GROUPS)):
                sp.wait_ge(k_rounded, g + 1)
                for half in range(BY_ACT[g], 2):
                    sp.dma_start(placed(g, half, half).bitcast(F32), packed(k_high[:, g % 2, :], g, half)
                                 ).then_inc(k_placed[g % 2], 16)
                sp.wait_ge(k_low, g + 1)
                for half in range(2):
                    sp.dma_start(placed(g, half, 1 - half).bitcast(F32), packed(room[:, g % K_SLOTS, :], g, half)
                                 ).then_inc(k_moved[g % K_SLOTS], 16)
                if g >= 1 and g - 1 + K_SLOTS < len(GROUPS):
                    sp.wait_ge(k_moved[(g - 1) % K_SLOTS], 32 * ((g - 1) // K_SLOTS + 1))
                    load_k(g - 1 + K_SLOTS)
            for t in range(2):
                load_dense(t)
            for s in range(K_SLOTS):
                sp.wait_ge(k_moved[s], 32 * len(range(s, len(GROUPS), K_SLOTS)))
            sp.dma_start(b1_sb[:, :], b1).then_inc(small_in, 16)
            sp.dma_start(b2_sb[:, :], b2).then_inc(small_in, 16)
            sp.dma_start(w3_sb[:, :], w3).then_inc(small_in, 16)
            sp.dma_start(w1_sb, w1).then_inc(w_in, 16)
            sp.dma_start(w2_sb, w2).then_inc(w_in, 16)
            for t in range(tiles):
                if t >= 2:
                    wait_z_free(sp, t)
                    load_dense(t)
                if t < tiles - 1:
                    sp.wait_ge(piece_taken, (t + 1) * len(pieces))
                else:
                    sp.wait_ge(tail_taken, TAIL_THREE)
                sp.dma_start(y[:, t * P:(t + 1) * P], y_row).then_inc(y_out, 16)
            sp.wait_ge(y_out, 16 * tiles)

        @block.gpsimd
        def _(pool):
            nc.gpsimd.memset(ident[:, :], 0.0).then_inc(ident_zero, 1)
            pool.wait_ge(ident_zero, 1)
            nc.gpsimd.affine_select(out=ident[:, :], in_=ident[:, :], pattern=[[-1, P]], compare_op=ALU.not_equal,
                                    fill=1.0, base=0, channel_multiplier=1).then_inc(ident_ready, 1)
            pool.wait_ge(ids_in, 16)

            def gather(t, fields):
                for f in fields:
                    c = t * FIELDS + f
                    nc.gpsimd.indirect_dma_start(
                        emb[t % 2][:, f, :], None, tables[f],
                        bass.IndirectOffsetOnAxis(idx[:, c:c + 1], 0)).then_inc(gathered[t % 2][f // QUAD], 16)

            def fold(c):
                pool.wait_ge(products, c + 1)
                x = products_of(c).rearrange("p (a e) -> p a e", e=E)
                half, quarter = E // 2, E // 4
                once = nc.gpsimd.tensor_tensor(x[:, :, 0:half], x[:, :, 0:half], x[:, :, half:E], ALU.add)
                if how[c] == "pool":
                    once.then_inc(partly["pool"], 1)
                else:
                    once.then_inc(halved, 1)
                    pool.wait_ge(halved, nth("pool4", c))
                    nc.gpsimd.tensor_tensor(x[:, :, 0:quarter], x[:, :, 0:quarter], x[:, :, quarter:half], ALU.add
                                            ).then_inc(partly["pool4"], 1)

            fields = [f for q in GATHER_ORDER for f in range(QUAD * q, QUAD * q + QUAD)]
            gather(0, fields)
            for t in range(tiles):
                if 1 <= t < tiles - 1:
                    pool.wait_ge(products, t * UNITS)
                for n in range(UNITS):
                    if how[t * UNITS + n] in LEFT:
                        fold(t * UNITS + n)
                    if t < tiles - 1:
                        gather(t + 1, fields[FIELDS * n // GATHER_UNITS:FIELDS * (n + 1) // GATHER_UNITS])

        @block.tensor
        def _(pe):
            pe.wait_ge(ident_ready, 1)
            quads_done, pieces_done = [0], [0]

            def transpose_quad():
                pe.wait_ge(quad_doubled, quads_done[0] + 1)
                pe.wait_ge(quad_low, quads_done[0])
                if pieces_done[0]:
                    pe.wait_ge(piece_taken, pieces_done[0])
                for r in range(QUAD):
                    x = twice[:, r, :, :].rearrange("p a e -> p (a e)")
                    last = nc.tensor.matmul(pT[:, r, :], x, ident[:, :], is_transpose=True, start=r == 0,
                                            stop=r == QUAD - 1)
                last.then_inc(quad_transposed, 1)
                quads_done[0] += 1
                return quads_done[0]

            def subtract_quad(t, q):
                if quads_done[0] == 1:
                    pe.wait_ge(minus_ready, 1)
                pe.wait_ge(quad_high, quads_done[0])
                s = QUAD * q % SLOTS
                nc.tensor.matmul(pT[:, :, :], minus_ident[:, :], xh[:, s:s + QUAD, :], start=False, stop=True,
                                 skip_group_check=True).then_inc(quad_left, 1)

            def unit(t, n, split_count):
                u = ORDER[n]
                count = t * UNITS + n
                if t == 0:
                    g = u["group"]
                    pe.wait_ge(k_placed[g % 2], 32 * (g // 2 + 1))
                    pe.wait_ge(k_moved[g % K_SLOTS], 32 * (g // K_SLOTS + 1))
                pe.wait_ge(quad_low, split_count)
                if count >= V_SLOTS:
                    pe.wait_ge(products, count - V_SLOTS + 1)
                out, at = v[count % V_SLOTS], u["at"] * E
                side, pos = u["side"], 0
                for _ in u["ks"]:
                    for _ in u["js"]:
                        slot = u["pairs"][pos // E][1] % SLOTS
                        width = side * E
                        spans = [(pos + o, min(512, width)) for o in range(0, width, 512)]
                        for part in (xh, xl):
                            for o, w in spans:
                                last = nc.tensor.matmul(out[:, o:o + w], part[:, slot, :], kk[:, at + o:at + o + w],
                                                        start=part is xh, stop=part is xl)
                        pos += width
                last.then_inc(v_ready, 1)

            to_sum = []

            def sum_parts(most):
                groups = E // PARTS
                for c, g in to_sum[:most]:
                    if g == 0:
                        pe.wait_ge(products, c + 1)
                        if nth("pe", c) > 1:
                            pe.wait_ge(summed["pe"], nth("pe", c) - 1)
                    x = products_of(c).rearrange("p (a g s) -> p a g s", g=groups, s=PARTS)
                    out = partial[:, 0:UNIT * PARTS].rearrange("p (a s) -> p a s", s=PARTS)
                    last = nc.tensor.matmul(out, ident[:, :], x[:, :, g, :], start=g == 0, stop=g == groups - 1)
                    if g == groups - 1:
                        last.then_inc(partly["pe"], 1)
                del to_sum[:most]

            def layer_chunk(out, w, x, chunks, n, width=P):
                for c in range(chunks):
                    last = nc.tensor.matmul(out, w[:, c, n * width:(n + 1) * width], x[:, c, :],
                                            start=c == 0, stop=c == chunks - 1)
                return last

            def piece(t, i):
                kind, n = pieces[i]
                count = t * len(pieces) + i
                base = t * len(pieces)
                out = pT[:, 0, :]
                pe.wait_ge(quad_low, quads_done[0])
                if count:
                    pe.wait_ge(piece_taken, count)
                pieces_done[0] = count + 1
                if i == 0:
                    wait_z(pe, t)
                    pe.wait_ge(dense_in[t % 2], 16 * (t // 2 + 1))
                if i == ONE and t == 0:
                    pe.wait_ge(w_in, 32)
                    pe.wait_ge(small_in, 48)
                if i in (ONE, TWO, THREE):
                    pe.wait_ge(piece_taken, base + i)
                if kind == "turn":
                    last = nc.tensor.transpose(out, z[t % 2][:, n * P:(n + 1) * P], ident[:, :])
                elif kind == "one":
                    last = layer_chunk(out, w1_sb, zT, c0, n)
                elif kind == "two":
                    last = layer_chunk(out, w2_sb, h1T, c1, n)
                else:
                    last = layer_chunk(out[0:1, :], w3_sb[:, :].unsqueeze(2), h2T, c2, 0, 1)
                last.then_inc(piece_made, 1)

            def due(c):
                if c >= V_SLOTS and how[c - V_SLOTS] == "pe":
                    to_sum.extend((c - V_SLOTS, g) for g in range(E // PARTS))

            split_at = {}
            for t in range(tiles):
                for n in range(UNITS):
                    c = t * UNITS + n
                    for what, which in pt_before[c]:
                        if what == "turn":
                            split_at[which] = transpose_quad()
                        else:
                            subtract_quad(*which)
                    if t == 0:
                        due(c)
                        sum_parts(PE_GROUPS)
                    unit(t, n, max(split_at[t, j // QUAD] for _, j in ORDER[n]["pairs"]))
                    if t >= 1:
                        due(c)
                        sum_parts(PE_GROUPS)
                    for what, which in pt_after[c]:
                        if what == "split":
                            subtract_quad(*which)
                        else:
                            piece(*which)
            t = tiles - 1
            z_last = z[t % 2]
            pe.wait_ge(piece_taken, t * len(pieces))
            for kind in kinds:
                if nth(kind, t * UNITS + early_unit):
                    pe.wait_ge(summed[kind], nth(kind, t * UNITS + early_unit))
            for c in range(early):
                last = nc.tensor.matmul(pT[:, c, :], z_last[:, c * P:(c + 1) * P], ident[:, :], is_transpose=True,
                                        start=c == 0, stop=c == early - 1)
            last.then_inc(tail_made, 1)
            pe.wait_ge(tail_taken, EARLY_TURNS)
            pe.wait_ge(products, tiles * UNITS - V_SLOTS + 1)
            for n in range(c1):
                for c in range(early):
                    nc.tensor.matmul(one_out[:, n, :], w1_sb[:, c, n * P:(n + 1) * P], zT[:, c, :],
                                     start=n == 0 and c == 0, stop=False, skip_group_check=True)
            for c in range(tiles * UNITS - V_SLOTS, tiles * UNITS):
                if how[c] == "pe":
                    to_sum.extend((c, g) for g in range(E // PARTS))
            sum_parts(len(to_sum))
            wait_z(pe, t)
            pe.wait_ge(dense_in[t % 2], 16 * (t // 2 + 1))
            nc.tensor.transpose(pT[:, early, :], z_last[:, early * P:zd], ident[:, :]).then_inc(tail_made, 1)
            pe.wait_ge(tail_taken, LAST_TURN)
            for n in range(c1):
                last = nc.tensor.matmul(one_out[:, n, :], w1_sb[:, early, n * P:(n + 1) * P], zT[:, early, :],
                                        start=False, stop=True, skip_group_check=True)
            last.then_inc(tail_made, 1)
            for c in range(c1):
                pe.wait_ge(tail_taken, TAIL_ONE + c)
                for n in range(c2):
                    last = nc.tensor.matmul(two_out[n], w2_sb[:, c, n * P:(n + 1) * P], h1T[:, c, :],
                                            start=c == 0, stop=c == c1 - 1)
                    if c == c1 - 1:
                        last.then_inc(tail_made, 1)
            for c in range(c2):
                pe.wait_ge(tail_taken, TAIL_TWO + c)
                last = nc.tensor.matmul(pT[0:1, 0, :], w3_sb[:, c:c + 1], h2T[:, c, :], start=c == 0, stop=c == c2 - 1)
            last.then_inc(tail_made, 1)

        @block.scalar
        def _(act):
            def round_k(g):
                act.wait_ge(k_in[g % K_SLOTS], 16 * (g // K_SLOTS + 1))
                if g >= 2:
                    act.wait_ge(k_low, g - 1)
                    act.wait_ge(k_placed[g % 2], 32 * (g // 2))
                cols = group_cols(g)
                nc.scalar.activation(k_high[:, g % 2, 0:cols].bitcast(F32R), room[:, g % K_SLOTS, 0:cols], ACT.Copy
                                     ).then_inc(k_rounded, 1)
                if BY_ACT[g]:
                    act.wait_ge(k_rounded, g + 1)
                for half in range(BY_ACT[g]):
                    nc.scalar.activation(placed(g, half, half), packed(k_high[:, g % 2, :], g, half), ACT.Copy
                                         ).then_inc(k_placed[g % 2], 16)

            def double_quad(i):
                t, q = quads[i]
                act.wait_ge(gathered[t % 2][q], 16 * QUAD * (t // 2 + 1))
                act.wait_ge(quad_transposed, i)
                x = emb[t % 2][:, QUAD * q:QUAD * q + QUAD, :].unsqueeze(2).broadcast_to([P, QUAD, 2, E])
                nc.scalar.activation(twice[:, :, :, :], x, ACT.Copy).then_inc(quad_doubled, 1)

            quads_done = [0]

            def round_quad(t, q):
                act.wait_ge(quad_transposed, quads_done[0] + 1)
                done = (t - 1) * UNITS + LAST_USE[q + 4] + 1 if q < 4 else t * UNITS + LAST_USE[q - 4] + 1
                if done > 0:
                    act.wait_ge(v_ready, done)
                s = QUAD * q % SLOTS
                nc.scalar.activation(xh[:, s:s + QUAD, :], pT[:, :, :], ACT.Copy).then_inc(quad_high, 1)
                quads_done[0] += 1

            def low_quad(t, q):
                act.wait_ge(quad_left, quads_done[0])
                s = QUAD * q % SLOTS
                nc.scalar.activation(xl[:, s:s + QUAD, :], pT[:, :, :], ACT.Copy).then_inc(quad_low, 1)

            doubled = [0]

            def double_due(c):
                if doubled[0] == quads_done[0] and doubled[0] < len(quads) and unit_of[doubled[0]] <= c + DOUBLE_AHEAD:
                    double_quad(doubled[0])
                    doubled[0] += 1

            to_sum = []

            def sum_up(most):
                for c, a in to_sum[:most]:
                    u = ORDER[c % UNITS]
                    if a == 0:
                        act.wait_ge(products, c + 1)
                        wait_z_free(act, c // UNITS)
                    e = products_of(c)[:, a * E:(a + 1) * E]
                    at = u["at"] + a
                    last = nc.scalar.activation(e, e, ACT.Copy, accum_out=z[c // UNITS % 2][:, at:at + 1])
                    if a == UNIT - 1:
                        last.then_inc(summed["act"], 1)
                del to_sum[:most]

            def take_piece(t, i):
                kind, n = pieces[i]
                count = t * len(pieces) + i
                x = pT[:, 0, :]
                if count == 0:
                    act.wait_ge(small_in, 48)
                act.wait_ge(piece_made, count + 1)
                if kind == "turn":
                    last = nc.scalar.activation(zT[:, n, :], x, ACT.Copy)
                elif kind == "one":
                    if t >= 1 and n == 0:
                        act.wait_ge(y_out, 16 * t)
                    last = nc.scalar.activation(h1T[:, n, :], x, ACT.Relu, bias=b1_sb[:, n:n + 1])
                elif kind == "two":
                    last = nc.scalar.activation(h2T[:, n, :], x, ACT.Relu, bias=b2_sb[:, n:n + 1])
                else:
                    last = nc.scalar.activation(y_row, x[0:1, :], ACT.Copy)
                last.then_inc(piece_taken, 1)

            next_group = [0]

            def rounds(c):
                while next_group[0] < len(GROUPS) and K_AT[next_group[0]] <= c:
                    round_k(next_group[0])
                    next_group[0] += 1

            act.wait_ge(ident_ready, 1)
            nc.scalar.activation(minus_ident[:, :], ident[:, :], ACT.Copy, scale=-1.0).then_inc(minus_ready, 1)
            rounds(-1)
            double_due(0)
            for t in range(tiles):
                for n in range(UNITS):
                    c = t * UNITS + n
                    for what, which in pt_before[c]:
                        if what == "turn":
                            double_due(c)
                            round_quad(*which)
                        else:
                            low_quad(*which)
                    if t == 0:
                        rounds(c)
                    double_due(c)
                    if c >= ACT_LAG and how[c - ACT_LAG] == "act":
                        to_sum.extend((c - ACT_LAG, a) for a in range(UNIT))
                    sum_up(ACT_PAIRS)
                    double_due(c)
                    for what, which in pt_after[c]:
                        if what == "split":
                            low_quad(*which)
                        else:
                            take_piece(*which)
            for c in range(tiles * UNITS - ACT_LAG, tiles * UNITS):
                if how[c] == "act":
                    to_sum.extend((c, a) for a in range(UNIT))
            act.wait_ge(tail_made, EARLY_TURNS)
            nc.scalar.activation(zT[:, 0:early, :], pT[:, 0:early, :], ACT.Copy).then_inc(tail_taken, 1)
            sum_up(len(to_sum))
            act.wait_ge(tail_made, LAST_TURN)
            nc.scalar.activation(zT[:, early, :], pT[:, early, :], ACT.Copy).then_inc(tail_taken, 1)
            act.wait_ge(tail_made, LAST_TURN + 1)
            act.wait_ge(y_out, 16 * (tiles - 1))
            for n in range(c1):
                nc.scalar.activation(h1T[:, n, :], one_out[:, n, :], ACT.Relu, bias=b1_sb[:, n:n + 1]
                                     ).then_inc(tail_taken, 1)
            for n in range(c2):
                act.wait_ge(tail_made, LAST_TURN + 2 + n)
                nc.scalar.activation(h2T[:, n, :], two_out[n], ACT.Relu, bias=b2_sb[:, n:n + 1]
                                     ).then_inc(tail_taken, 1)
            act.wait_ge(tail_made, LAST_TURN + 2 + c2)
            nc.scalar.activation(y_row, pT[0:1, 0, :], ACT.Copy).then_inc(tail_taken, 1)

        @block.vector
        def _(dve):
            def low_k(g):
                dve.wait_ge(k_rounded, g + 1)
                cols = group_cols(g)
                raw = room[:, g % K_SLOTS, 0:cols]
                nc.vector.tensor_tensor(raw, raw, k_high[:, g % 2, 0:cols], ALU.subtract
                                        ).then_inc(k_low, 1)

            seen = [set() for _ in range(tiles)]

            def multiply(t, n):
                u = ORDER[n]
                count = t * UNITS + n
                side, ks, js = u["side"], u["ks"], u["js"]
                cols = len(u["pairs"]) * E
                dve.wait_ge(v_ready, count + 1)
                if t == 1 and n == 0:
                    for s in range(2):
                        dve.wait_ge(k_placed[s], 32 * len(range(s, len(GROUPS), 2)))
                    last_slot = K_SLOTS - 1
                    dve.wait_ge(k_moved[last_slot], 32 * len(range(last_slot, len(GROUPS), K_SLOTS)))
                wait_slot(dve, count)
                for q in sorted({i // QUAD for i, _ in u["pairs"]} - seen[t]):
                    dve.wait_ge(gathered[t % 2][q], 16 * QUAD * (t // 2 + 1))
                    seen[t].add(q)
                i0 = u["pairs"][0][0]
                x = emb[t % 2][:, i0:i0 + 2 * side * len(ks), :].rearrange(
                    "p (k s) e -> p k (s e)", k=len(ks))[:, :, 0:side * E]
                x = x.unsqueeze(2).broadcast_to([P, len(ks), len(js), side * E])
                shape = dict(k=len(ks), j=len(js))
                nc.vector.tensor_tensor(
                    products_of(count)[:, 0:cols].rearrange("p (k j c) -> p k j c", **shape),
                    v[count % V_SLOTS][:, 0:cols].rearrange("p (k j c) -> p k j c", **shape),
                    x, ALU.mult).then_inc(products, 1)

            def finish(c):
                u, kind = ORDER[c % UNITS], how[c]
                pairs = len(u["pairs"])
                if kind == "dve":
                    dve.wait_ge(products, c + 1)
                    x = products_of(c)[:, 0:pairs * E].rearrange("p (a e) -> p a e", e=E)
                else:
                    dve.wait_ge(partly[kind], nth(kind, c))
                    if kind in LEFT:
                        x = products_of(c).rearrange("p (a e) -> p a e", e=E)[:, :, 0:LEFT[kind]]
                    else:
                        x = partial[:, 0:UNIT * PARTS].rearrange("p (a s) -> p a s", s=PARTS)
                nc.vector.tensor_reduce(z[c // UNITS % 2][:, u["at"]:u["at"] + pairs], x, AX_X, ALU.add
                                        ).then_inc(summed[kind], 1)

            next_group = [0]

            def lows(c):
                while next_group[0] < len(GROUPS) and LOW_AT[next_group[0]] <= c:
                    low_k(next_group[0])
                    next_group[0] += 1

            lows(-1)
            z_seen = set()
            units = tiles * UNITS
            for c in range(units + max(LAG.values())):
                t, n = divmod(c, UNITS)
                if c < units:
                    if t == 0:
                        lows(c)
                    multiply(t, n)
                for kind, lag in LAG.items():
                    if lag <= c < units + lag and how[c - lag] == kind:
                        if (c - lag) // UNITS not in z_seen:
                            wait_z_free(dve, (c - lag) // UNITS)
                            z_seen.add((c - lag) // UNITS)
                        finish(c - lag)


def kernel(**inputs):
    import concourse.bacc as bacc
    from concourse.bass_utils import run_bass_kernel_spmd

    def chunks(a):
        a = np.asarray(a)
        return np.ascontiguousarray(a.reshape(a.shape[0] // P, P, -1).transpose(1, 0, 2))

    ids = np.asarray(inputs["ids"])
    tiles = ids.shape[0] // P
    k = np.asarray(inputs["L0_rec_kernel"])[:, STORED_TO_TRIU, :].reshape(E, PAIRS * E)
    k_raw = np.concatenate([np.concatenate([k[:, group[half]["at"] * E:][:, :len(group[half]["pairs"]) * E]
                                            for group in GROUPS], axis=1) for half in range(2)], axis=0)
    w1 = np.asarray(inputs["W_top1"])
    rows = np.concatenate([STORED_TO_TRIU, np.arange(PAIRS, w1.shape[0])])

    arrays = {
        "ids": np.ascontiguousarray(ids.reshape(tiles, P, FIELDS).transpose(1, 0, 2).reshape(P, -1)),
        "dense": np.asarray(inputs["dense_ctx"]),
        "k_raw": np.ascontiguousarray(k_raw),
        "w1": chunks(w1[rows]),
        "b1": np.ascontiguousarray(np.asarray(inputs["b_top1"]).reshape(-1, P).T),
        "w2": chunks(inputs["W_top2"]),
        "b2": np.ascontiguousarray(np.asarray(inputs["b_top2"]).reshape(-1, P).T),
        "w3": np.ascontiguousarray(np.asarray(inputs["W_top3"]).reshape(-1, P).T),
    }
    for f in range(FIELDS):
        arrays[f"tbl_{f}"] = np.asarray(inputs[f"tbl_{f}"])
    nc = bacc.Bacc("TRN2", target_bir_lowering=False, num_devices=1)
    dram = {n: nc.dram_tensor(n, a.shape, mybir.dt.from_np(a.dtype), kind="ExternalInput").ap()
            for n, a in arrays.items()}
    y = nc.dram_tensor("y", (1, tiles * P), F32, kind="ExternalOutput").ap()
    interaction_tower(nc, dram["ids"], dram["dense"], [dram[f"tbl_{f}"] for f in range(FIELDS)], dram["k_raw"],
                      dram["w1"], dram["b1"], dram["w2"], dram["b2"], dram["w3"], y)
    result = run_bass_kernel_spmd(nc, [arrays], core_ids=[0])
    return result.results[0]["y"].reshape(tiles * P, 1)
```
